# Optimizing a Trainium2 kernel written in Bass

```python
import numpy as np
import jax
import jax.numpy as jnp

def _softmax(x, axis=-1):
    return jax.nn.softmax(x, axis=axis)

def _gelu(x):
    return jax.nn.gelu(x, approximate=True)

def _silu(x):
    return jax.nn.silu(x)

def _sigmoid(x):
    return jax.nn.sigmoid(x)

def _layernorm(x, axis=-1, eps=1e-05):
    m = jnp.mean(x, axis=axis, keepdims=True)
    v = jnp.var(x, axis=axis, keepdims=True)
    return (x - m) / jnp.sqrt(v + eps)

def _scatter_add(tgt, idx, src, axis=0):
    return tgt.at[idx].add(src)

def _segment_sum(src, seg, n):
    return jax.ops.segment_sum(src, seg, n)
kernel_name = 'mk_adaln_ffn_d2_seqx_r4_25f96d'

def setup_inputs(seed: int=0):
    np.random.seed(seed)
    _w = jnp.asarray

    def _rec_inputs():
        import jax
        import jax.numpy as jnp
        _rk = jax.random.key(seed)
        x = -7.109e-05 + 0.9999 * jax.random.normal(jax.random.fold_in(_rk, 1), (64, 64, 512), jnp.float32)
        _lenS = 64 - jax.random.randint(jax.random.fold_in(_rk, 7), (64,), 0, max(1, 64 // 4) + 1, jnp.int32)
        _lenS2 = 64 - jax.random.randint(jax.random.fold_in(_rk, 8), (64,), 0, max(1, 64 // 4) + 1, jnp.int32)
        itok_B_1_198 = jax.random.randint(jax.random.fold_in(_rk, 11), (64,), 1, 199, jnp.int32)
        itok_B_0_6 = jax.random.randint(jax.random.fold_in(_rk, 12), (64,), 0, 7, jnp.int32)
        return (x, itok_B_1_198, itok_B_0_6)
    x, itok_B_1_198, itok_B_0_6 = _rec_inputs()

    def _L0_cond_setup():
        import jax, jax.numpy as jnp
        import numpy as np
        B, C, T = (128, 64, 512)
        S, D = (200, 64)
        key = jax.random.key(seed)
        k1, k2, k3 = jax.random.split(key, 3)
        x = jax.random.normal(k1, (B, C, T), dtype=jnp.float32)
        conditions = jax.random.randint(k2, (B,), 0, S, dtype=jnp.int64)
        weights = jax.random.normal(k3, (S, C, D), dtype=jnp.float32) / jnp.sqrt(jnp.float32(C))
        return {'x': x, 'conditions': conditions, 'weights': weights}
    _L0_cond_all = _L0_cond_setup()
    _L0_cond_in = {k: v for k, v in _L0_cond_all.items() if k in ('weights',)}
    del _L0_cond_all

    def _L0_ffn_setup():
        import jax, jax.numpy as jnp
        import numpy as np
        HIDDEN = 512
        INTER = 1408
        B, S = (2, 512)

        def _ternary(key, shape):
            return jax.random.randint(key, shape, -1, 2).astype(jnp.float32)
        key = jax.random.key(seed)
        ks = jax.random.split(key, 7)
        x = jax.random.normal(ks[0], (B, S, HIDDEN), dtype=jnp.float32)
        gate_w = _ternary(ks[1], (INTER, HIDDEN))
        up_w = _ternary(ks[2], (INTER, HIDDEN))
        down_w = _ternary(ks[3], (HIDDEN, INTER))
        gate_s = jax.random.uniform(ks[4], (INTER,), minval=0.01, maxval=0.1, dtype=jnp.float32)
        up_s = jax.random.uniform(ks[5], (INTER,), minval=0.01, maxval=0.1, dtype=jnp.float32)
        down_s = jax.random.uniform(ks[6], (HIDDEN,), minval=0.01, maxval=0.1, dtype=jnp.float32)
        return {'x': x, 'gate_w': gate_w, 'up_w': up_w, 'down_w': down_w, 'gate_s': gate_s, 'up_s': up_s, 'down_s': down_s}
    _L0_ffn_all = _L0_ffn_setup()
    _L0_ffn_in = {k: v for k, v in _L0_ffn_all.items() if k in ('gate_w', 'up_w', 'down_w', 'gate_s', 'up_s', 'down_s')}
    del _L0_ffn_all

    def _L1_cond_setup():
        import jax, jax.numpy as jnp
        import numpy as np
        B, T, D_IN, D_OUT = (16, 512, 512, 512)
        N_ADAPTERS, RANK = (8, 16)
        key = jax.random.key(seed)
        k_x, k_w, k_a, k_b, k_s, k_idx = jax.random.split(key, 6)
        x = jax.random.normal(k_x, (B, T, D_IN), dtype=jnp.float32)
        W = jax.random.normal(k_w, (D_OUT, D_IN), dtype=jnp.float32) * (1.0 / np.sqrt(D_IN))
        A = jax.random.normal(k_a, (N_ADAPTERS, RANK, D_IN), dtype=jnp.float32) * 0.02
        Bm = jax.random.normal(k_b, (N_ADAPTERS, D_OUT, RANK), dtype=jnp.float32) * 0.02
        scalings = jnp.ones((N_ADAPTERS,), dtype=jnp.float32)
        adapter_idx = jax.random.randint(k_idx, (B,), 0, N_ADAPTERS, dtype=jnp.int32)
        return {'x': x, 'W': W, 'A': A, 'Bm': Bm, 'scalings': scalings, 'adapter_idx': adapter_idx}
    _L1_cond_all = _L1_cond_setup()
    _L1_cond_in = {k: v for k, v in _L1_cond_all.items() if k in ('W', 'A', 'Bm', 'scalings')}
    del _L1_cond_all

    def _L1_ffn_setup():
        import jax, jax.numpy as jnp
        import numpy as np
        EPS = 1e-05

        def _ternary_weight(w, eps=EPS):
            alpha = jnp.maximum(jnp.mean(jnp.abs(w)), eps)
            return jnp.clip(jnp.round(w / alpha), -1.0, 1.0) * alpha

        def _absmax_act(x, eps=EPS):
            scale = jnp.maximum(jnp.max(jnp.abs(x), axis=-1, keepdims=True), eps) / 127.0
            return jnp.clip(jnp.round(x / scale), -128.0, 127.0) * scale
        key = jax.random.key(seed)
        k1, k2, k3 = jax.random.split(key, 3)
        B, S, D_IN, D_OUT = (4, 2048, 512, 512)
        x = jax.random.normal(k1, (B, S, D_IN), dtype=jnp.float32)
        bound_w = 1.0 / np.sqrt(D_IN)
        weight = jax.random.uniform(k2, (D_OUT, D_IN), dtype=jnp.float32, minval=-bound_w, maxval=bound_w)
        bias = jax.random.uniform(k3, (D_OUT,), dtype=jnp.float32, minval=-bound_w, maxval=bound_w)
        return {'x': x, 'weight': weight, 'bias': bias}
    _L1_ffn_all = _L1_ffn_setup()
    _L1_ffn_in = {k: v for k, v in _L1_ffn_all.items() if k in ('weight', 'bias')}
    del _L1_ffn_all
    return {'x': x, 'itok_B_1_198': itok_B_1_198, 'itok_B_0_6': itok_B_0_6, 'L0_cond_weights': _L0_cond_in['weights'], 'L0_ffn_gate_w': _L0_ffn_in['gate_w'], 'L0_ffn_up_w': _L0_ffn_in['up_w'], 'L0_ffn_down_w': _L0_ffn_in['down_w'], 'L0_ffn_gate_s': _L0_ffn_in['gate_s'], 'L0_ffn_up_s': _L0_ffn_in['up_s'], 'L0_ffn_down_s': _L0_ffn_in['down_s'], 'L1_cond_W': _L1_cond_in['W'], 'L1_cond_A': _L1_cond_in['A'], 'L1_cond_Bm': _L1_cond_in['Bm'], 'L1_cond_scalings': _L1_cond_in['scalings'], 'L1_ffn_weight': _L1_ffn_in['weight'], 'L1_ffn_bias': _L1_ffn_in['bias']}

def reference(x, itok_B_1_198, itok_B_0_6, L0_cond_weights, L0_ffn_gate_w, L0_ffn_up_w, L0_ffn_down_w, L0_ffn_gate_s, L0_ffn_up_s, L0_ffn_down_s, L1_cond_W, L1_cond_A, L1_cond_Bm, L1_cond_scalings, L1_ffn_weight, L1_ffn_bias):
    import jax
    import jax.numpy as jnp

    def _L0_cond_ref(x, conditions, weights):
        import jax, jax.numpy as jnp
        import numpy as np
        B, C, T = (128, 64, 512)
        S, D = (200, 64)
        w = weights[conditions]
        return jnp.einsum('bct,bcd->bdt', x, w)

    def _L0_ffn_ref(x, gate_w, up_w, down_w, gate_s, up_s, down_s):
        import jax, jax.numpy as jnp
        import numpy as np
        HIDDEN = 512
        INTER = 1408
        B, S = (2, 512)

        def _ternary(key, shape):
            return jax.random.randint(key, shape, -1, 2).astype(jnp.float32)
        b, s, h = x.shape
        xf = x.reshape(b * s, h)
        g = jnp.einsum('th,ih->ti', xf, gate_w) * gate_s
        u = jnp.einsum('th,ih->ti', xf, up_w) * up_s
        hdn = jax.nn.silu(g) * u
        out = jnp.einsum('ti,hi->th', hdn, down_w) * down_s
        return out.reshape(b, s, -1)

    def _L1_cond_ref(x, W, A, Bm, scalings, adapter_idx):
        import jax, jax.numpy as jnp
        import numpy as np
        B, T, D_IN, D_OUT = (16, 512, 512, 512)
        N_ADAPTERS, RANK = (8, 16)
        H = jnp.einsum('btd,od->bto', x, W)
        A_b = A[adapter_idx]
        B_b = Bm[adapter_idx]
        s_b = scalings[adapter_idx]
        xa = jnp.einsum('btd,brd->btr', x, A_b)
        delta = jnp.einsum('btr,bor->bto', xa, B_b)
        delta = jax.lax.stop_gradient(delta * s_b[:, None, None])
        return H + delta

    def _L1_ffn_ref(x, weight, bias):
        import jax, jax.numpy as jnp
        import numpy as np
        EPS = 1e-05

        def _ternary_weight(w, eps=EPS):
            alpha = jnp.maximum(jnp.mean(jnp.abs(w)), eps)
            return jnp.clip(jnp.round(w / alpha), -1.0, 1.0) * alpha

        def _absmax_act(x, eps=EPS):
            scale = jnp.maximum(jnp.max(jnp.abs(x), axis=-1, keepdims=True), eps) / 127.0
            return jnp.clip(jnp.round(x / scale), -128.0, 127.0) * scale
        q_w = _ternary_weight(weight).astype(x.dtype)
        q_x = _absmax_act(x)
        return jnp.einsum('bsi,oi->bso', q_x, q_w) + bias.astype(x.dtype)
    x = x + _L0_ffn_ref(_L0_cond_ref(x, itok_B_1_198, L0_cond_weights), L0_ffn_gate_w, L0_ffn_up_w, L0_ffn_down_w, L0_ffn_gate_s, L0_ffn_up_s, L0_ffn_down_s)
    x = x + _L1_ffn_ref(_L1_cond_ref(x, L1_cond_W, L1_cond_A, L1_cond_Bm, L1_cond_scalings, itok_B_0_6), L1_ffn_weight, L1_ffn_bias)
    return x

_drawn_inputs = setup_inputs


def setup_inputs(seed=0):
    import zlib

    import numpy as np

    out = dict(_drawn_inputs(seed))
    spreads = {'L1_cond_scalings': (1.0, 0.6)}
    factors = {'L1_cond_A': 3.62, 'L1_cond_Bm': 3.624, 'L1_ffn_bias': 4.419}
    for name, (base, spread) in spreads.items():
        noise = np.random.default_rng([zlib.crc32(name.encode()), seed]).standard_normal(out[name].shape)
        drawn = base * np.exp(spread * noise) if base else spread * noise
        out[name] = jnp.asarray(drawn.astype(out[name].dtype))
    for name, factor in factors.items():
        out[name] = (out[name] * factor).astype(out[name].dtype)
    return out
```

```python
from contextlib import ExitStack

import concourse.bass as bass
from concourse import mybir

ALU = mybir.AluOpType
ACT = mybir.ActivationFunctionType
AX = mybir.AxisListType
F32 = mybir.dt.float32
F32R = mybir.dt.float32r
BF16 = mybir.dt.bfloat16
I32 = mybir.dt.int32
RMAX = bass.bass_isa.ReduceOp.max
RADD = bass.bass_isa.ReduceOp.add

P = 128
LOW_BITS = 0xFFF
ROUND = 12582912.0
EPS = 1e-5


def adaln_ffn_kernel(nc, x_rows, x_cols, mix_idx, adapter_idx, mix_w, ffn0_w, gate_s, up_s, down_s,
                     w_t, a_t, b_t, scalings, qw_t, bias, out):
    BATCHES, C, D = x_rows.shape
    N_MIX = mix_w.shape[0]
    TILES = ffn0_w.shape[1]
    KD = D // P
    TOK = 512
    NB = TOK // C
    PAIRS = NB // 2
    CHUNKS = BATCHES // NB
    RANK = P // scalings.shape[0]
    H_AT, FFN_AT = 2, 7
    SCALE_AFTER, Q_AFTER = 3, (3, 4)

    with ExitStack() as ctx:
        def sb(name, shape, dt):
            return ctx.enter_context(nc.sbuf_tensor(name, shape, dt))

        def sem(name):
            return ctx.enter_context(nc.semaphore(name))

        ffn0 = sb("ffn0", [P, TILES, 3, D], F32R)
        w_hi = sb("w_hi", [P, KD, D], F32R)
        w_lo = sb("w_lo", [P, KD, D], F32R)
        a_hi = sb("a_hi", [P, KD, P], F32R)
        a_lo = sb("a_lo", [P, KD, P], F32R)
        b_hi = sb("b_hi", [P, D], F32R)
        b_lo = sb("b_lo", [P, D], F32R)
        qw = sb("qw", [P, KD, D], BF16)
        stage = sb("stage", [P, KD, D], F32)
        a_stage = sb("a_stage", [P, KD, P], F32)
        b_stage = sb("b_stage", [P, D], F32)

        xr = sb("xr", [P, PAIRS, D], F32)
        mixw = sb("mixw", [P, PAIRS, P], F32)
        y_hi = sb("y_hi", [P, KD, TOK], F32R)
        y_lo = sb("y_lo", [P, KD, TOK], F32R)
        gated = sb("gated", [P, 2, TOK], F32)
        hid = sb("hid", [P, 2, TOK], F32)
        hid_hi = sb("hid_hi", [P, 2, TOK], F32R)
        hid_lo = sb("hid_lo", [P, 2, TOK], F32R)
        xc = sb("xc", [P, KD, TOK], F32)
        x1_hi = sb("x1_hi", [P, KD, TOK], F32R)
        x1_lo = sb("x1_lo", [P, KD, TOK], F32R)
        xa = sb("xa", [P, TOK], F32)
        xa_hi = sb("xa_hi", [P, TOK], F32R)
        xa_lo = sb("xa_lo", [P, TOK], F32R)
        h = sb("h", [P, KD, TOK], F32)
        amax = sb("amax", [P, TOK], F32)
        amax_all = sb("amax_all", [P, TOK], F32)
        scale = sb("scale", [P, TOK], F32)
        rscale = sb("rscale", [P, TOK], F32)
        q = sb("q", [P, KD, TOK], BF16)
        deq = sb("deq", [P, 2, TOK], F32)

        gs = sb("gs", [P, TILES], F32)
        us = sb("us", [P, TILES], F32)
        ds = sb("ds", [P, KD], F32)
        bs = sb("bs", [P, KD], F32)
        mix_i = sb("mix_i", [1, BATCHES], I32)
        ad_i = sb("ad_i", [P, BATCHES], I32)
        ad_f = sb("ad_f", [P, BATCHES], F32)
        scal = sb("scal", [P, P // RANK], F32)
        part_i = sb("part_i", [P, 2], I32)
        nums_i = sb("nums_i", [P, P // RANK], I32)
        own_i = sb("own_i", [P, 1], F32)
        nums = sb("nums", [P, P // RANK], F32)
        own = sb("own", [P, P // RANK], F32)
        own_s = sb("own_s", [P, 1], F32)
        mask = sb("mask", [P, BATCHES], F32)
        inexact = sb("inexact", [P, TILES], F32)
        inexact_to = sb("inexact_to", [P, TILES], F32)
        flags = sb("flags", [P, TILES], F32)
        tile_stage = [h[:, 0:3, :], xc[:, 0:3, :]]
        raw = nc.dram_tensor("raw", (P, TILES, 3, D), F32).ap()
        wsum = sb("wsum", [P, 4], F32)

        bank = [ctx.enter_context(nc.psum_tensor(f"bank{n}", [P, TOK], F32)) for n in range(4)]
        acc = [ctx.enter_context(nc.psum_tensor(f"acc{m}", [P, TOK], F32)) for m in range(KD)]

        small_in = sem("small_in")
        mix_idx_in = sem("mix_idx_in")
        ab_in = sem("ab_in")
        w_in = sem("w_in")
        qw_in = sem("qw_in")
        tile_in = [sem(f"tile_in{i}") for i in range(TILES)]
        raw_copied = [sem(f"raw_copied{i}") for i in range(TILES)]
        raw_in = [sem(f"raw_in{i}") for i in range(TILES)]
        xr_in = sem("xr_in")
        mixw_in = sem("mixw_in")
        xc_in = [sem(f"xc_in{m}") for m in range(KD)]
        stored = [sem(f"stored{m}") for m in range(KD)]
        mix_done = sem("mix_done")
        gate_done = sem("gate_done")
        up_done = sem("up_done")
        down_tile = sem("down_tile")
        acc_done = sem("acc_done")
        xa_done = sem("xa_done")
        h_done = sem("h_done")
        ffn_done = sem("ffn_done")
        y_hi_done = sem("y_hi_done")
        silu_done = sem("silu_done")
        hid_hi_done = sem("hid_hi_done")
        x1_hi_done = sem("x1_hi_done")
        xa_hi_done = sem("xa_hi_done")
        h_out = sem("h_out")
        tile_kept = sem("tile_kept")
        w_hi_done = sem("w_hi_done")
        mixw_zero = sem("mixw_zero")
        mask_step = sem("mask_step")
        low_done = sem("low_done")
        inexact_done = sem("inexact_done")
        tested = sem("tested")
        y_lo_done = sem("y_lo_done")
        hid_done = sem("hid_done")
        x1_done = sem("x1_done")
        xa_masked = sem("xa_masked")
        amax_done = sem("amax_done")
        scale_done = sem("scale_done")
        rscale_done = sem("rscale_done")
        q_scaled = sem("q_scaled")
        q_clipped = sem("q_clipped")
        q_done = sem("q_done")
        deq_done = sem("deq_done")
        out_done = sem("out_done")
        wsum_done = sem("wsum_done")
        alpha_done = sem("alpha_done")
        qw_step = sem("qw_step")
        qw_done = sem("qw_done")
        iota_done = sem("iota_done")
        flag_done = sem("flag_done")
        hid_lo_done = sem("hid_lo_done")
        x1_lo_done = sem("x1_lo_done")
        xa_lo_done = sem("xa_lo_done")
        amax_all_done = sem("amax_all_done")
        w_lo_done = sem("w_lo_done")
        wsum_all = sem("wsum_all")

        xr_dram = x_rows.rearrange("(g q b) c t -> g (b c) q t", q=PAIRS, b=2)
        mix_idx_dram = mix_idx.rearrange("(a b) -> a b", a=1)

        def tok(c):
            return bass.ds(c * TOK, TOK)

        block = ctx.enter_context(nc.Block())

        @block.sync
        def _(sp):
            def load_mix(c):
                sp.dma_start(xr[:], xr_dram[bass.ds(c, 1)].rearrange("a p q t -> (a p) q t")).then_inc(xr_in, 16)
                for j in range(NB):
                    w = sp.value_load(mix_i[0:1, bass.ds(c * NB + j, 1)], min_val=0, max_val=N_MIX - 1)
                    half = slice(C * (j % 2), C * (j % 2) + C)
                    sp.dma_start(mixw[half, j // 2, half],
                                 mix_w[bass.ds(w, 1)].rearrange("a c d -> (a c) d")).then_inc(mixw_in, 16)

            def load_cols(c, m):
                sp.dma_start(xc[:, m, :], x_cols[m * P:(m + 1) * P, tok(c)]).then_inc(xc_in[m], 16)

            def store(c):
                for m in range(KD):
                    sp.wait_ge(out_done, KD * c + m + 1)
                    sp.dma_start(out[m * P:(m + 1) * P, tok(c)], xc[:, m, :]).then_inc(stored[m], 16)

            def load_tile(i):
                if i >= 2:
                    sp.wait_ge(tested, i - 1)
                sp.dma_start(tile_stage[i % 2], ffn0_w[:, i]
                             ).then_inc(tile_in[i], 16)

            def load_raw(i):
                sp.wait_ge(flag_done, i + 1)
                low_bits = sp.value_load(flags[0:1, i:i + 1].bitcast(I32))
                with sp.If(low_bits != 0):
                    sp.dma_start(raw[:, i], ffn0_w[:, i]).then_inc(raw_copied[i], 16)
                    sp.wait_ge(raw_copied[i], 16)
                    sp.dma_start(ffn0[:, i].bitcast(F32), raw[:, i]
                                 ).then_inc(raw_in[i], 16)
                with sp.Else():
                    sp.nop()

            sp.dma_start(mix_i[:], mix_idx_dram).then_inc(mix_idx_in, 16)
            load_tile(0)
            sp.wait_ge(mix_idx_in, 16)
            sp.wait_ge(mixw_zero, 1)
            load_mix(0)
            load_tile(1)
            sp.dma_start(stage[:], w_t).then_inc(w_in, 16)
            sp.wait_ge(mix_done, KD)
            load_mix(1)
            for i in range(TILES):
                if i >= 2:
                    load_tile(i)
                    load_raw(i - 2)
            for m in range(KD):
                if m == 0:
                    sp.wait_ge(tested, TILES - 1)
                load_cols(0, m)
            load_raw(TILES - 2)
            sp.wait_ge(w_lo_done, KD)
            sp.dma_start(stage[:], qw_t).then_inc(qw_in, 16)
            load_raw(TILES - 1)

            def steady(c, last):
                if not last:
                    sp.wait_ge(mix_done, (c + 1) * KD)
                    load_mix(c + 1)
                store(c - 1)
                for m in range(KD):
                    sp.wait_ge(stored[m], c * 16)
                    load_cols(c, m)

            with sp.Fori(1, CHUNKS - 1) as c:
                steady(c, False)
            steady(CHUNKS - 1, True)
            store(CHUNKS - 1)
            for m in range(KD):
                sp.wait_ge(stored[m], CHUNKS * 16)

        @block.tensor
        def _(pe):
            def mix(c):
                pe.wait_ge(xr_in, (c + 1) * 16)
                pe.wait_ge(mixw_in, (c + 1) * 16 * NB)
                for t, b in enumerate((2, 3, 0, 1)):
                    for pair in range(PAIRS):
                        mm = pe.matmul(bank[b][:, pair * P:(pair + 1) * P], xr[:, pair, t * P:(t + 1) * P],
                                       mixw[:, pair, :], start=True, stop=True)
                    mm.then_inc(mix_done, 1)

            def mix_banks_free(c):
                pe.wait_ge(silu_done, (c + 1) * TILES)
                pe.wait_ge(hid_done, (c + 1) * TILES)

            def split_products(psum, lhs, hi, lo, exact, first, last):
                n = len(lhs)
                for k in range(n):
                    for part in (hi[k], lo[k]):
                        mm = pe.matmul(psum, lhs[k][exact], part if exact else part.bitcast(F32),
                                       start=first and k == 0 and part is hi[k],
                                       stop=last and k == n - 1 and part is lo[k])
                return mm

            def weight(i, which, k):
                w = ffn0[:, i, which, k * P:(k + 1) * P]
                return w.bitcast(F32), w

            ys_hi = [y_hi[:, k, :] for k in range(KD)]
            ys_lo = [y_lo[:, k, :] for k in range(KD)]

            def gate_up(i, exact):
                a, b = 2 * (i % 2), 2 * (i % 2) + 1
                split_products(bank[a][:], [weight(i, 0, k) for k in range(KD)], ys_hi, ys_lo, exact,
                               True, True).then_inc(gate_done, 1)
                return a, b

            def up(i, b, exact):
                split_products(bank[b][:], [weight(i, 1, k) for k in range(KD)], ys_hi, ys_lo, exact,
                               True, True).then_inc(up_done, 1)

            def down(c, i, exact):
                pe.wait_ge(hid_lo_done, c * TILES + i + 1)
                for m in range(KD):
                    mm = split_products(acc[m][:], [weight(i, 2, m)], [hid_hi[:, i % 2, :]], [hid_lo[:, i % 2, :]],
                                        exact, i == 0, i == TILES - 1)
                    if i == TILES - 1:
                        mm.then_inc(acc_done, 1)
                if i < TILES - 1:
                    mm.then_inc(down_tile, 1)

            def three(psum, whi, wlo, hi, lo, first, last):
                pe.matmul(psum, whi, hi, start=first, stop=False)
                pe.matmul(psum, whi, lo, start=False, stop=False)
                return pe.matmul(psum, wlo, hi, start=False, stop=last)

            def adapter_down(c, silu_now):
                pe.wait_ge(x1_lo_done, (c + 1) * KD)
                pe.wait_ge(silu_done, silu_now)
                for k in range(KD):
                    mm = three(bank[0][:], a_hi[:, k, :], a_lo[:, k, :], x1_hi[:, k, :], x1_lo[:, k, :],
                               k == 0, k == KD - 1)
                mm.then_inc(xa_done, 1)

            def h_tile(c, m):
                b = (1, 2, 3, 1)[m]
                cols = slice(m * P, (m + 1) * P)
                for k in range(KD):
                    three(bank[b][:], w_hi[:, k, cols], w_lo[:, k, cols], x1_hi[:, k, :], x1_lo[:, k, :],
                          k == 0, False)
                if m == 0:
                    pe.wait_ge(xa_lo_done, c + 1)
                three(bank[b][:], b_hi[:, cols], b_lo[:, cols], xa_hi[:], xa_lo[:], False, True).then_inc(h_done, 1)

            def ffn_tile(c, m):
                b = (2, 3, 0, 1)[m]
                for k in range(KD):
                    if m == 0 and k % 2 == 0:
                        pe.wait_ge(q_done, 2 * c + k // 2 + 1)
                    mm = pe.matmul(bank[b][:], qw[:, k, m * P:(m + 1) * P], q[:, k, :],
                                   start=(k == 0), stop=(k == KD - 1))
                mm.then_inc(ffn_done, 1)

            def chunk(c, last, exact):
                n = c * TILES
                for i in range(TILES):
                    if i == H_AT:
                        adapter_down(c - 1, n + 1)
                        pe.wait_ge(hid_done, n + 1)
                        h_tile(c - 1, 0)
                        pe.wait_ge(silu_done, n + 2)
                        h_tile(c - 1, 1)
                        pe.wait_ge(hid_done, n + 2)
                        h_tile(c - 1, 2)
                        pe.wait_ge(h_out, (c - 1) * KD + 1)
                        h_tile(c - 1, 3)
                    if i == FFN_AT:
                        pe.wait_ge(hid_done, n + 6)
                        ffn_tile(c - 1, 0)
                        ffn_tile(c - 1, 1)
                        pe.wait_ge(silu_done, n + 7)
                        ffn_tile(c - 1, 2)
                        pe.wait_ge(hid_done, n + 7)
                        ffn_tile(c - 1, 3)
                    if i == 0:
                        pe.wait_ge(y_lo_done, (c + 1) * KD)
                    elif i == H_AT:
                        pe.wait_ge(xa_masked, c)
                    elif i == H_AT + 1:
                        pe.wait_ge(h_out, (c - 1) * KD + 2)
                    elif i == FFN_AT:
                        pe.wait_ge(deq_done, (c - 1) * KD + 1)
                    elif i == FFN_AT + 1:
                        pe.wait_ge(deq_done, (c - 1) * KD + 3)
                    elif i > 1:
                        pe.wait_ge(silu_done, n + i - 1)
                    a, b = gate_up(i, exact)
                    if i == H_AT:
                        pe.wait_ge(h_out, (c - 1) * KD + 4)
                    elif i == H_AT + 1:
                        pe.wait_ge(h_out, (c - 1) * KD + 3)
                    elif i == FFN_AT:
                        pe.wait_ge(deq_done, (c - 1) * KD + 2)
                    elif i == FFN_AT + 1:
                        pe.wait_ge(deq_done, (c - 1) * KD + 4)
                    elif i > 1:
                        pe.wait_ge(hid_done, n + i - 1)
                    up(i, b, exact)
                    if i == 1:
                        pe.wait_ge(x1_done, c * KD)
                    if i >= 1:
                        down(c, i - 1, exact)
                if not last:
                    mix_banks_free(c)
                    mix(c + 1)
                down(c, TILES - 1, exact)

            mix(0)
            for i in range(TILES):
                pe.wait_ge(flag_done, i + 1)
                low_bits = pe.value_load(flags[0:1, i:i + 1].bitcast(I32))
                if i == 0:
                    pe.wait_ge(y_lo_done, KD)
                if i > 1:
                    pe.wait_ge(hid_done, i - 1)

                def tile(exact):
                    a, b = gate_up(i, exact)
                    up(i, b, exact)
                    if i >= 1:
                        down(0, i - 1, exact)
                with pe.If(low_bits == 0):
                    tile(True)
                with pe.Else():
                    pe.wait_ge(raw_in[i], 16)
                    tile(False)
            mix_banks_free(0)
            mix(1)
            with pe.If(low_bits == 0):
                down(0, TILES - 1, True)
            with pe.Else():
                down(0, TILES - 1, False)

            pe.wait_ge(w_lo_done, KD + 2)
            pe.wait_ge(qw_done, 1)
            with pe.Fori(1, CHUNKS - 1) as c:
                with pe.If(low_bits == 0):
                    chunk(c, False, True)
                with pe.Else():
                    chunk(c, False, False)
            with pe.If(low_bits == 0):
                chunk(CHUNKS - 1, True, True)
            with pe.Else():
                chunk(CHUNKS - 1, True, False)

            c = CHUNKS - 1
            adapter_down(c, CHUNKS * TILES)
            pe.wait_ge(hid_done, CHUNKS * TILES)
            for m in range(KD):
                if m == KD - 1:
                    pe.wait_ge(h_out, c * KD + 1)
                h_tile(c, m)
            pe.wait_ge(h_out, (c + 1) * KD)
            for m in range(KD):
                ffn_tile(c, m)

        @block.scalar
        def _(act):
            for dst, src in ((gs[:], gate_s), (us[:], up_s), (ds[:], down_s), (bs[:], bias)):
                act.dma_start(dst, src).then_inc(small_in, 16)
            act.dma_start(ad_i[:], adapter_idx.rearrange("(a b) -> a b", a=1).broadcast_to([P, BATCHES])
                          ).then_inc(small_in, 16)
            act.dma_start(scal[:], scalings.rearrange("(a b) -> a b", a=1).broadcast_to([P, P // RANK])
                          ).then_inc(small_in, 16)
            act.dma_start(a_stage[:], a_t).then_inc(ab_in, 16)
            act.dma_start(b_stage[:], b_t).then_inc(ab_in, 16)

            def y_high(c):
                for t, b in enumerate((2, 3, 0, 1)):
                    act.wait_ge(mix_done, c * KD + t + 1)
                    act.activation(y_hi[:, t, :], bank[b][:], ACT.Copy).then_inc(y_hi_done, 1)

            def silu(c, i, first):
                act.wait_ge(gate_done, c * TILES + i + 1)
                if not (first and i < 2):
                    act.wait_ge(hid_done, c * TILES + max(i - 1, 0))
                act.activation(gated[:, i % 2, :], bank[2 * (i % 2)][:], ACT.Silu,
                               scale=gs[:, i:i + 1]).then_inc(silu_done, 1)

            def hid_high(c, i, first):
                act.wait_ge(hid_done, c * TILES + i + 1)
                if i < 2 and not first:
                    act.wait_ge(acc_done, c * KD)
                elif i >= 2:
                    act.wait_ge(down_tile, c * (TILES - 1) + i - 1)
                act.activation(hid_hi[:, i % 2, :], hid[:, i % 2, :], ACT.Copy).then_inc(hid_hi_done, 1)

            def keep_tile(i):
                act.wait_ge(tile_in[i], 16)
                act.activation(ffn0[:, i], tile_stage[i % 2], ACT.Copy).then_inc(tile_kept, 1)

            def x1_high(c):
                for m in range(KD):
                    act.wait_ge(x1_done, c * KD + m + 1)
                    act.activation(x1_hi[:, m, :], xc[:, m, :], ACT.Copy).then_inc(x1_hi_done, 1)

            def second_layer(c):
                act.wait_ge(xa_masked, c + 1)
                act.activation(xa_hi[:], xa[:], ACT.Copy).then_inc(xa_hi_done, 1)
                for m in range(KD):
                    act.wait_ge(h_done, c * KD + m + 1)
                    act.activation(h[:, m, :], bank[(1, 2, 3, 1)[m]][:], ACT.Copy).then_inc(h_out, 1)

            def chunk(c, last):
                for i in range(TILES):
                    if i == 0:
                        x1_high(c - 1)
                    if i == H_AT:
                        second_layer(c - 1)
                    silu(c, i, False)
                    hid_high(c, i, False)
                if not last:
                    y_high(c + 1)

            act.wait_ge(small_in, 16 * 6)
            keep_tile(0)
            y_high(0)
            keep_tile(1)
            for i in range(TILES):
                silu(0, i, True)
                hid_high(0, i, True)
                if i + 2 < TILES:
                    keep_tile(i + 2)
                if 4 <= i < 4 + KD:
                    if i == 4:
                        act.wait_ge(w_in, 16)
                    act.activation(w_hi[:, i - 4, :], stage[:, i - 4, :], ACT.Copy).then_inc(w_hi_done, 1)
                if i == 8:
                    act.wait_ge(ab_in, 32)
                    act.activation(a_hi[:], a_stage[:], ACT.Copy).then_inc(w_hi_done, 1)
                if i == 9:
                    act.activation(b_hi[:], b_stage[:], ACT.Copy).then_inc(w_hi_done, 1)
            y_high(1)
            with act.Fori(1, CHUNKS - 1) as c:
                chunk(c, False)
            chunk(CHUNKS - 1, True)
            x1_high(CHUNKS - 1)
            second_layer(CHUNKS - 1)

        @block.vector
        def _(dve):
            def y_low(c):
                for t, b in enumerate((2, 3, 0, 1)):
                    dve.wait_ge(y_hi_done, c * KD + t + 1)
                    dve.tensor_tensor(y_lo[:, t, :], bank[b][:], y_hi[:, t, :].bitcast(F32),
                                      ALU.subtract).then_inc(y_lo_done, 1)

            def hidden(c, i, first):
                dve.wait_ge(up_done, c * TILES + i + 1)
                dve.wait_ge(silu_done, c * TILES + i + 1)
                if not (first and i < 2):
                    dve.wait_ge(hid_lo_done, c * TILES + max(i - 1, 0))
                dve.scalar_tensor_tensor(out=hid[:, i % 2, :], in0=bank[2 * (i % 2) + 1][:], scalar=us[:, i:i + 1],
                                         in1=gated[:, i % 2, :], op0=ALU.mult, op1=ALU.mult
                                         ).then_inc(hid_done, 1)

            def x1(c):
                for m in range(KD):
                    dve.wait_ge(acc_done, c * KD + m + 1)
                    dve.wait_ge(xc_in[m], (c + 1) * 16)
                    dve.scalar_tensor_tensor(out=xc[:, m, :], in0=acc[m][:], scalar=ds[:, m:m + 1],
                                             in1=xc[:, m, :], op0=ALU.mult, op1=ALU.add).then_inc(x1_done, 1)

            def xa_mask(c):
                dve.wait_ge(xa_done, c + 1)
                of_batch = mask[:, bass.ds(c * NB, NB)].rearrange("p (b a) -> p b a", a=1).broadcast_to([P, NB, C])
                dve.tensor_tensor(xa[:].rearrange("p (b d) -> p b d", d=C),
                                  bank[0][:].rearrange("p (b d) -> p b d", d=C), of_batch,
                                  ALU.mult).then_inc(xa_masked, 1)

            def h_max(c):
                dve.wait_ge(h_out, (c + 1) * KD)
                dve.tensor_reduce(amax[:], h[:].rearrange("p m n -> p n m"), AX.X, ALU.max,
                                  apply_absolute_value=True).then_inc(amax_done, 1)

            def h_scale(c):
                dve.wait_ge(amax_all_done, c + 1)
                dve.tensor_scalar(scale[:], amax_all[:], EPS, 1.0 / 127.0, ALU.max, ALU.mult
                                  ).then_inc(scale_done, 1)
                dve.wait_ge(scale_done, c + 1)
                dve.reciprocal(rscale[:], scale[:]).then_inc(rscale_done, 1)

            def quantise(c, half):
                ms = slice(2 * half, 2 * half + 2)
                n = 2 * c + half + 1
                dve.wait_ge(rscale_done, c + 1)
                every = rscale[:].rearrange("p (a n) -> p a n", a=1).broadcast_to([P, 2, TOK])
                dve.tensor_tensor(h[:, ms, :], h[:, ms, :], every, ALU.mult).then_inc(q_scaled, 1)
                dve.wait_ge(q_scaled, n)
                dve.tensor_scalar(h[:, ms, :], h[:, ms, :], 127.0, -128.0, ALU.min, ALU.max).then_inc(q_clipped, 1)
                dve.wait_ge(q_clipped, n)
                dve.tensor_scalar(q[:, ms, :], h[:, ms, :], ROUND, ROUND, ALU.add, ALU.subtract).then_inc(q_done, 1)

            def result(c):
                for m in range(KD):
                    dve.wait_ge(ffn_done, c * KD + m + 1)
                    dve.scalar_tensor_tensor(out=deq[:, m % 2, :], in0=bank[(2, 3, 0, 1)[m]][:], scalar=wsum[:, 2:3],
                                             in1=scale[:], op0=ALU.mult, op1=ALU.mult).then_inc(deq_done, 1)
                    dve.wait_ge(deq_done, c * KD + m + 1)
                    dve.scalar_tensor_tensor(out=xc[:, m, :], in0=deq[:, m % 2, :], scalar=bs[:, m:m + 1],
                                             in1=xc[:, m, :], op0=ALU.add, op1=ALU.add).then_inc(out_done, 1)

            def test_tile(i):
                low = tile_stage[i % 2].bitcast(I32)
                dve.wait_ge(tile_kept, i + 1)
                dve.tensor_scalar(low, low, LOW_BITS, None, ALU.bitwise_and).then_inc(low_done, 1)
                dve.wait_ge(low_done, i + 1)
                dve.tensor_reduce(inexact[:, i:i + 1], low, AX.XY, ALU.max).then_inc(inexact_done, 1)
                dve.wait_ge(inexact_done, i + 1)
                dve.tensor_reduce(inexact_to[:, i:i + 1], inexact[:, 0:i + 1], AX.X, ALU.max).then_inc(tested, 1)

            def chunk(c, last):
                x1(c - 1)
                for i in range(TILES):
                    if i == H_AT:
                        xa_mask(c - 1)
                        h_max(c - 1)
                    if i == FFN_AT:
                        result(c - 1)
                    hidden(c, i, False)
                    if i == SCALE_AFTER:
                        h_scale(c - 1)
                    for half in range(2):
                        if i == Q_AFTER[half]:
                            quantise(c - 1, half)
                if not last:
                    y_low(c + 1)

            dve.memset(mixw[:], 0.0).then_inc(mixw_zero, 1)

            dve.wait_ge(iota_done, 2)
            dve.wait_ge(small_in, 16 * 6)
            dve.tensor_scalar(part_i[:, 1:2], part_i[:, 0:1], RANK.bit_length() - 1, None,
                              ALU.arith_shift_right).then_inc(mask_step, 1)
            dve.tensor_copy(nums[:], nums_i[:]).then_inc(mask_step, 1)
            dve.tensor_copy(ad_f[:], ad_i[:]).then_inc(mask_step, 1)
            dve.wait_ge(mask_step, 3)
            dve.tensor_copy(own_i[:], part_i[:, 1:2]).then_inc(mask_step, 1)
            dve.wait_ge(mask_step, 4)
            dve.scalar_tensor_tensor(out=own[:], in0=nums[:], scalar=own_i[:, 0:1], in1=scal[:],
                                     op0=ALU.is_equal, op1=ALU.mult).then_inc(mask_step, 1)
            dve.wait_ge(mask_step, 5)
            dve.tensor_reduce(own_s[:], own[:], AX.X, ALU.add).then_inc(mask_step, 1)
            dve.wait_ge(mask_step, 6)
            dve.tensor_scalar(mask[:], ad_f[:], own_i[:, 0:1], own_s[:, 0:1], ALU.is_equal, ALU.mult
                              ).then_inc(mask_step, 1)
            dve.wait_ge(mask_step, 7)

            test_tile(0)
            y_low(0)
            test_tile(1)
            for i in range(TILES):
                hidden(0, i, True)
                if i + 2 < TILES:
                    test_tile(i + 2)
                if i == 9:
                    dve.wait_ge(qw_in, 16)
                    dve.tensor_reduce(wsum[:, 0:1], stage[:], AX.XY, ALU.add, apply_absolute_value=True
                                      ).then_inc(wsum_done, 1)
            y_low(1)
            dve.wait_ge(wsum_all, 1)
            dve.tensor_scalar(wsum[:, 2:3], wsum[:, 1:2], 1.0 / (D * D), EPS, ALU.mult, ALU.max
                              ).then_inc(alpha_done, 1)
            dve.wait_ge(alpha_done, 1)
            dve.reciprocal(wsum[:, 3:4], wsum[:, 2:3]).then_inc(alpha_done, 1)
            dve.wait_ge(alpha_done, 2)
            dve.tensor_scalar(stage[:], stage[:], wsum[:, 3:4], 1.0, ALU.mult, ALU.min).then_inc(qw_step, 1)
            dve.wait_ge(qw_step, 1)
            dve.tensor_scalar(stage[:], stage[:], -1.0, ROUND, ALU.max, ALU.add).then_inc(qw_step, 1)
            dve.wait_ge(qw_step, 2)
            dve.tensor_scalar(qw[:], stage[:], -ROUND, None, ALU.add).then_inc(qw_done, 1)

            with dve.Fori(1, CHUNKS - 1) as c:
                chunk(c, False)
            chunk(CHUNKS - 1, True)
            c = CHUNKS - 1
            x1(c)
            xa_mask(c)
            h_max(c)
            h_scale(c)
            quantise(c, 0)
            quantise(c, 1)
            result(c)

        @block.gpsimd
        def _(pool):
            def hid_low(c, i, first):
                pool.wait_ge(hid_hi_done, c * TILES + i + 1)
                pool.tensor_tensor(hid_lo[:, i % 2, :], hid[:, i % 2, :], hid_hi[:, i % 2, :].bitcast(F32),
                                   ALU.subtract).then_inc(hid_lo_done, 1)

            def x1_low(c):
                for m in range(KD):
                    pool.wait_ge(x1_hi_done, c * KD + m + 1)
                    pool.tensor_tensor(x1_lo[:, m, :], xc[:, m, :], x1_hi[:, m, :].bitcast(F32),
                                       ALU.subtract).then_inc(x1_lo_done, 1)

            def second_layer(c):
                pool.wait_ge(xa_hi_done, c + 1)
                pool.tensor_tensor(xa_lo[:], xa[:], xa_hi[:].bitcast(F32), ALU.subtract).then_inc(xa_lo_done, 1)
                pool.wait_ge(wsum_all, 1)
                pool.wait_ge(amax_done, c + 1)
                pool.partition_all_reduce(amax_all[:], amax[:], P, RMAX).then_inc(amax_all_done, 1)

            def flag(i):
                pool.wait_ge(tested, i + 1)
                pool.partition_all_reduce(flags[:, i:i + 1], inexact_to[:, i:i + 1], P, RMAX).then_inc(flag_done, 1)

            def chunk(c):
                x1_low(c - 1)
                for i in range(TILES):
                    if i == H_AT:
                        second_layer(c - 1)
                    hid_low(c, i, False)

            pool.iota(part_i[:, 0:1], pattern=[[0, 1]], base=0, channel_multiplier=1).then_inc(iota_done, 1)
            pool.iota(nums_i[:], pattern=[[1, P // RANK]], base=0, channel_multiplier=0).then_inc(iota_done, 1)
            flag(0)
            flag(1)
            for i in range(TILES):
                hid_low(0, i, True)
                if i + 2 < TILES:
                    flag(i + 2)
                if 4 <= i < 4 + KD:
                    k = i - 4
                    pool.wait_ge(w_hi_done, k + 1)
                    pool.tensor_tensor(w_lo[:, k, :], stage[:, k, :], w_hi[:, k, :].bitcast(F32),
                                       ALU.subtract).then_inc(w_lo_done, 1)
                if i == 8:
                    pool.wait_ge(w_hi_done, KD + 1)
                    pool.tensor_tensor(a_lo[:], a_stage[:], a_hi[:].bitcast(F32), ALU.subtract).then_inc(w_lo_done, 1)
                if i == 9:
                    pool.wait_ge(w_hi_done, KD + 2)
                    pool.tensor_tensor(b_lo[:], b_stage[:], b_hi[:].bitcast(F32), ALU.subtract).then_inc(w_lo_done, 1)
            pool.wait_ge(wsum_done, 1)
            pool.partition_all_reduce(wsum[:, 1:2], wsum[:, 0:1], P, RADD).then_inc(wsum_all, 1)
            with pool.Fori(1, CHUNKS) as c:
                chunk(c)
            x1_low(CHUNKS - 1)
            second_layer(CHUNKS - 1)


def kernel(x, itok_B_1_198, itok_B_0_6, L0_cond_weights, L0_ffn_gate_w, L0_ffn_up_w, L0_ffn_down_w, L0_ffn_gate_s,
           L0_ffn_up_s, L0_ffn_down_s, L1_cond_W, L1_cond_A, L1_cond_Bm, L1_cond_scalings, L1_ffn_weight, L1_ffn_bias):
    import numpy as np
    import concourse.bacc as bacc
    from concourse.bass_utils import run_bass_kernel_spmd

    a = np.asarray
    batches, chans, d = x.shape
    kd, tiles = d // P, L0_ffn_gate_w.shape[0] // P

    def rows_in(w):
        return a(w).T.reshape(kd, P, -1).transpose(1, 0, 2)

    def by_tile(w):
        return a(w).reshape(tiles, P, kd, P).transpose(3, 0, 2, 1).reshape(P, tiles, d)

    down = a(L0_ffn_down_w).reshape(kd, P, tiles, P).transpose(3, 2, 0, 1).reshape(P, tiles, d)
    ins = {
        "x_rows": a(x),
        "x_cols": a(x).transpose(2, 0, 1).reshape(d, batches * chans),
        "mix_idx": a(itok_B_1_198),
        "adapter_idx": a(itok_B_0_6),
        "mix_w": a(L0_cond_weights),
        "ffn0_w": np.stack([by_tile(L0_ffn_gate_w), by_tile(L0_ffn_up_w), down], axis=2),
        "gate_s": a(L0_ffn_gate_s).reshape(tiles, P).T,
        "up_s": a(L0_ffn_up_s).reshape(tiles, P).T,
        "down_s": a(L0_ffn_down_s).reshape(kd, P).T,
        "w_t": rows_in(L1_cond_W),
        "a_t": rows_in(a(L1_cond_A).reshape(P, d)),
        "b_t": a(L1_cond_Bm).transpose(0, 2, 1).reshape(P, d),
        "scalings": a(L1_cond_scalings),
        "qw_t": rows_in(L1_ffn_weight),
        "bias": a(L1_ffn_bias).reshape(kd, P).T,
    }
    nc = bacc.Bacc("TRN2", target_bir_lowering=False, num_devices=1)
    arrays, args = {}, []
    for name, v in ins.items():
        v = np.ascontiguousarray(v)
        arrays[name] = v
        args.append(nc.dram_tensor(name, v.shape, mybir.dt.from_np(v.dtype), kind="ExternalInput").ap())
    args.append(nc.dram_tensor("out", (d, batches * chans), F32, kind="ExternalOutput").ap())
    adaln_ffn_kernel(nc, *args)
    r = run_bass_kernel_spmd(nc, [arrays], core_ids=[0])
    return r.results[0]["out"].reshape(d, batches, chans).transpose(1, 2, 0)
```

```python
from contextlib import ExitStack

import concourse.bass as bass
from concourse import mybir

ALU = mybir.AluOpType
ACT = mybir.ActivationFunctionType
AX = mybir.AxisListType
F32 = mybir.dt.float32
F32R = mybir.dt.float32r
BF16 = mybir.dt.bfloat16
I32 = mybir.dt.int32
RMAX = bass.bass_isa.ReduceOp.max
RADD = bass.bass_isa.ReduceOp.add

P = 128
LOW_BITS = 0xFFF
ROUND = 12582912.0
EPS = 1e-5


def adaln_ffn_kernel(nc, x_rows, x_cols, mix_idx, adapter_idx, mix_w, ffn0_w, gate_s, up_s, down_s,
                     w_t, a_t, b_t, scalings, qw_t, bias, out):
    BATCHES, C, D = x_rows.shape
    N_MIX = mix_w.shape[0]
    TILES = ffn0_w.shape[1]
    KD = D // P
    TOK = 512
    NB = TOK // C
    PAIRS = NB // 2
    CHUNKS = BATCHES // NB
    RANK = P // scalings.shape[0]
    H_AT, FFN_AT = 2, 7
    SCALE_AFTER, Q_AFTER = 3, (3, 4)
    GROUPS = ((0,), (1,), (2,), (3, 4), (5, 6), (7, 8), (9, 10))
    TEST_AFTER = {0: (2,), 1: (3, 4), 2: (5,), 3: (6,), 4: (7,), 5: (8,), 6: (9,), 7: (10,)}
    HALF = TOK // 2
    MIX_BANKS = (2, 3, 0, 1)
    H_BANKS = (1, 2, 3, 1)
    FFN_BANKS = (2, 3, 0, 1)

    with ExitStack() as ctx:
        def sb(name, shape, dt):
            return ctx.enter_context(nc.sbuf_tensor(name, shape, dt))

        def sem(name):
            return ctx.enter_context(nc.semaphore(name))

        ffn0 = sb("ffn0", [P, TILES, 3, D], F32R)
        w_hi = sb("w_hi", [P, KD, D], F32R)
        w_lo = sb("w_lo", [P, KD, D], F32R)
        a_hi = sb("a_hi", [P, KD, P], F32R)
        a_lo = sb("a_lo", [P, KD, P], F32R)
        b_hi = sb("b_hi", [P, D], F32R)
        b_lo = sb("b_lo", [P, D], F32R)
        qw = sb("qw", [P, KD, D], BF16)
        w_stage = sb("w_stage", [P, KD, D], F32)
        a_stage = sb("a_stage", [P, KD, P], F32)
        b_stage = sb("b_stage", [P, D], F32)

        xr = sb("xr", [P, PAIRS, D], F32)
        mixw = sb("mixw", [P, PAIRS, P], F32)
        y_hi = sb("y_hi", [P, KD, TOK], F32R)
        y_lo = sb("y_lo", [P, KD, TOK], F32R)
        gated = sb("gated", [P, 2, TOK], F32)
        hid = sb("hid", [P, 2, TOK], F32)
        hid_hi = sb("hid_hi", [P, 2, TOK], F32R)
        hid_lo = sb("hid_lo", [P, 2, TOK], F32R)
        xc = sb("xc", [P, KD, TOK], F32)
        x1_hi = sb("x1_hi", [P, KD, TOK], F32R)
        x1_lo = sb("x1_lo", [P, KD, TOK], F32R)
        xa = sb("xa", [P, TOK], F32)
        xa_hi = sb("xa_hi", [P, TOK], F32R)
        xa_lo = sb("xa_lo", [P, TOK], F32R)
        h = sb("h", [P, KD, TOK], F32)
        per_token = sb("per_token", [P, 4, TOK], F32)
        amax = per_token[:, 0, :]
        amax_all = per_token[:, 1, :]
        scale = per_token[:, 2, :]
        rscale = per_token[:, 3, :]
        q_stage = per_token
        q = sb("q", [P, KD, TOK], BF16)
        deq = sb("deq", [P, 2, TOK], F32)

        gs = sb("gs", [P, TILES], F32)
        us = sb("us", [P, TILES], F32)
        ds = sb("ds", [P, KD], F32)
        bs = sb("bs", [P, KD], F32)
        mix_i = sb("mix_i", [1, BATCHES], I32)
        ad_i = sb("ad_i", [P, BATCHES], I32)
        ad_f = sb("ad_f", [P, BATCHES], F32)
        scal = sb("scal", [P, P // RANK], F32)
        part_i = sb("part_i", [P, 2], I32)
        nums_i = sb("nums_i", [P, P // RANK], I32)
        own_i = sb("own_i", [P, 1], F32)
        nums = sb("nums", [P, P // RANK], F32)
        own = sb("own", [P, P // RANK], F32)
        own_s = sb("own_s", [P, 1], F32)
        mask = sb("mask", [P, BATCHES], F32)
        inexact = sb("inexact", [P, TILES], F32)
        inexact_to = sb("inexact_to", [P, TILES], F32)
        flags = sb("flags", [P, TILES], F32)
        tile_stage = [h[:, 0:3, :], xc[:, 0:3, :], w_stage[:, 0:3, :]]
        STAGES = len(tile_stage)
        raw = nc.dram_tensor("raw", (P, TILES, 3, D), F32).ap()
        silu_warm = sb("silu_warm", [P, 1], F32)
        wsum = sb("wsum", [P, 4], F32)

        bank = [ctx.enter_context(nc.psum_tensor(f"bank{n}", [P, TOK], F32)) for n in range(4)]
        acc = [ctx.enter_context(nc.psum_tensor(f"acc{m}", [P, TOK], F32)) for m in range(KD)]

        small_in = sem("small_in")
        mix_idx_in = sem("mix_idx_in")
        ab_in = sem("ab_in")
        w_in = sem("w_in")
        qw_in = sem("qw_in")
        tile_in = [sem(f"tile_in{i}") for i in range(TILES)]
        raw_copied = [sem(f"raw_copied{i}") for i in range(TILES)]
        raw_in = [sem(f"raw_in{i}") for i in range(TILES)]
        xr_in = sem("xr_in")
        mixw_in = [sem(f"mixw_in{pair}") for pair in range(PAIRS)]
        xc_in = [sem(f"xc_in{m}") for m in range(KD)]
        stored = [sem(f"stored{m}") for m in range(KD)]
        mix_done = sem("mix_done")
        gate_done = sem("gate_done")
        up_done = sem("up_done")
        down_tile = sem("down_tile")
        acc_done = sem("acc_done")
        xa_done = sem("xa_done")
        h_done = sem("h_done")
        ffn_done = sem("ffn_done")
        y_hi_done = sem("y_hi_done")
        silu_done = sem("silu_done")
        hid_hi_done = sem("hid_hi_done")
        x1_hi_done = sem("x1_hi_done")
        xa_hi_done = sem("xa_hi_done")
        h_out = sem("h_out")
        tile_kept = sem("tile_kept")
        silu_ready = sem("silu_ready")
        w_hi_done = sem("w_hi_done")
        mixw_zero = sem("mixw_zero")
        mask_step = sem("mask_step")
        low_done = sem("low_done")
        inexact_done = sem("inexact_done")
        tested = sem("tested")
        y_lo_done = sem("y_lo_done")
        hid_done = sem("hid_done")
        x1_done = sem("x1_done")
        x1_lo_odd = sem("x1_lo_odd")
        xa_masked = sem("xa_masked")
        amax_done = sem("amax_done")
        scale_done = sem("scale_done")
        rscale_done = sem("rscale_done")
        q_scaled = sem("q_scaled")
        q_clipped = sem("q_clipped")
        q_done = sem("q_done")
        deq_done = sem("deq_done")
        out_done = sem("out_done")
        wsum_done = sem("wsum_done")
        alpha_done = sem("alpha_done")
        qw_step = sem("qw_step")
        qw_done = sem("qw_done")
        warm_zero = sem("warm_zero")
        iota_done = sem("iota_done")
        flag_done = sem("flag_done")
        hid_lo_done = sem("hid_lo_done")
        x1_lo_done = sem("x1_lo_done")
        xa_lo_done = sem("xa_lo_done")
        amax_all_done = sem("amax_all_done")
        w_lo_done = sem("w_lo_done")
        wsum_all = sem("wsum_all")

        xr_dram = x_rows.rearrange("(g q b) c t -> g (b c) q t", q=PAIRS, b=2)
        mix_idx_dram = mix_idx.rearrange("(a b) -> a b", a=1)

        def tok(c):
            return bass.ds(c * TOK, TOK)

        def toks_of(half):
            return slice(half * HALF, (half + 1) * HALF)

        def last_bank(half, m):
            return (acc, bank)[half][m][:, 0:HALF]

        def load_mix_weight(eng, c, j):
            w = eng.value_load(mix_i[0:1, bass.ds(c * NB + j, 1)], min_val=0, max_val=N_MIX - 1)
            half = slice(C * (j % 2), C * (j % 2) + C)
            eng.dma_start(mixw[half, j // 2, half],
                          mix_w[bass.ds(w, 1)].rearrange("a c d -> (a c) d")).then_inc(mixw_in[j // 2], 16)

        block = ctx.enter_context(nc.Block())

        @block.sync
        def _(sp):
            def load_rows(c):
                sp.dma_start(xr[:], xr_dram[bass.ds(c, 1)].rearrange("a p q t -> (a p) q t")).then_inc(xr_in, 16)

            def load_mix(c):
                load_rows(c)
                for j in range(NB):
                    load_mix_weight(sp, c, j)

            def load_cols(c, m):
                sp.dma_start(xc[:, m, :], x_cols[m * P:(m + 1) * P, tok(c)]).then_inc(xc_in[m], 16)

            def store(c):
                for m in range(KD):
                    sp.wait_ge(out_done, KD * c + m + 1)
                    sp.dma_start(out[m * P:(m + 1) * P, tok(c)], xc[:, m, :]).then_inc(stored[m], 16)

            def load_tile(i):
                if i >= STAGES:
                    sp.wait_ge(tested, i - STAGES + 1)
                sp.dma_start(tile_stage[i % STAGES], ffn0_w[:, i]
                             ).then_inc(tile_in[i], 16)

            def load_raw(i):
                sp.wait_ge(flag_done, i + 1)
                low_bits = sp.value_load(flags[0:1, i:i + 1].bitcast(I32))
                with sp.If(low_bits != 0):
                    sp.dma_start(raw[:, i], ffn0_w[:, i]).then_inc(raw_copied[i], 16)
                    sp.wait_ge(raw_copied[i], 16)
                    sp.dma_start(ffn0[:, i].bitcast(F32), raw[:, i]
                                 ).then_inc(raw_in[i], 16)
                with sp.Else():
                    sp.nop()

            sp.dma_start(mix_i[:], mix_idx_dram).then_inc(mix_idx_in, 16)
            load_rows(0)
            load_tile(0)
            sp.wait_ge(mix_idx_in, 16)
            sp.wait_ge(mixw_zero, 1)
            for j in range(NB // 2):
                load_mix_weight(sp, 0, j)
            load_tile(1)
            load_tile(2)
            sp.dma_start(q_stage[:], qw_t).then_inc(qw_in, 16)
            for i in range(STAGES, TILES):
                load_tile(i)
                load_raw(i - STAGES)
            sp.wait_ge(tested, TILES - 2)
            sp.dma_start(w_stage[:], w_t).then_inc(w_in, 16)
            load_raw(TILES - STAGES)
            sp.wait_ge(mix_done, KD)
            load_mix(1)
            sp.wait_ge(tested, TILES)
            for m in range(KD):
                load_cols(0, m)
            for i in range(TILES - STAGES + 1, TILES):
                load_raw(i)

            def steady(c, last):
                if not last:
                    sp.wait_ge(mix_done, (c + 1) * KD)
                    load_mix(c + 1)
                store(c - 1)
                for m in range(KD):
                    sp.wait_ge(stored[m], c * 16)
                    load_cols(c, m)

            with sp.Fori(1, CHUNKS - 1) as c:
                steady(c, False)
            steady(CHUNKS - 1, True)
            c = CHUNKS - 1
            for half in range(2):
                for m in range(KD):
                    sp.wait_ge(out_done, (c + half) * KD + m + 1)
                    sp.dma_start(out[m * P:(m + 1) * P, bass.ds(c * TOK + half * HALF, HALF)],
                                 xc[:, m, toks_of(half)]).then_inc(stored[m], 16)
            for m in range(KD):
                sp.wait_ge(stored[m], (CHUNKS + 1) * 16)

        @block.tensor
        def _(pe):
            def mix_product(t, pair):
                return pe.matmul(bank[MIX_BANKS[t]][:, pair * P:(pair + 1) * P], xr[:, pair, t * P:(t + 1) * P],
                                 mixw[:, pair, :], start=True, stop=True)

            def first_mix():
                pe.wait_ge(xr_in, 16)
                for pair in range(PAIRS):
                    pe.wait_ge(mixw_in[pair], 2 * 16)
                    for t in range(KD):
                        mm = mix_product(t, pair)
                        if pair == PAIRS - 1:
                            mm.then_inc(mix_done, 1)

            def mix(c):
                pe.wait_ge(xr_in, (c + 1) * 16)
                for pair in range(PAIRS):
                    pe.wait_ge(mixw_in[pair], (c + 1) * 2 * 16)
                for t in range(KD):
                    if t == 0:
                        pe.wait_ge(hid_done, c * TILES - 1)
                    if t == 2:
                        pe.wait_ge(silu_done, c * TILES)
                    if t == 3:
                        pe.wait_ge(hid_done, c * TILES)
                    for pair in range(PAIRS):
                        mm = mix_product(t, pair)
                    mm.then_inc(mix_done, 1)

            def split_products(psum, lhs, hi, lo, exact, first, last):
                n = len(lhs)
                for k in range(n):
                    for part in (hi[k], lo[k]):
                        mm = pe.matmul(psum, lhs[k][exact], part if exact else part.bitcast(F32),
                                       start=first and k == 0 and part is hi[k],
                                       stop=last and k == n - 1 and part is lo[k])
                return mm

            def weight(i, which, k):
                w = ffn0[:, i, which, k * P:(k + 1) * P]
                return w.bitcast(F32), w

            ys_hi = [y_hi[:, k, :] for k in range(KD)]
            ys_lo = [y_lo[:, k, :] for k in range(KD)]

            def gate_up(i, exact):
                a, b = 2 * (i % 2), 2 * (i % 2) + 1
                split_products(bank[a][:], [weight(i, 0, k) for k in range(KD)], ys_hi, ys_lo, exact,
                               True, True).then_inc(gate_done, 1)
                return a, b

            def up(i, b, exact):
                split_products(bank[b][:], [weight(i, 1, k) for k in range(KD)], ys_hi, ys_lo, exact,
                               True, True).then_inc(up_done, 1)

            def down(c, i, exact):
                pe.wait_ge(hid_lo_done, c * TILES + i + 1)
                for m in range(KD):
                    mm = split_products(acc[m][:], [weight(i, 2, m)], [hid_hi[:, i % 2, :]], [hid_lo[:, i % 2, :]],
                                        exact, i == 0, i == TILES - 1)
                    if i == TILES - 1:
                        mm.then_inc(acc_done, 1)
                if i < TILES - 1:
                    mm.then_inc(down_tile, 1)

            def three(psum, whi, wlo, hi, lo, first, last):
                pe.matmul(psum, whi, hi, start=first, stop=False)
                pe.matmul(psum, whi, lo, start=False, stop=False)
                return pe.matmul(psum, wlo, hi, start=False, stop=last)

            def adapter_down(c, silu_now, last):
                pe.wait_ge(silu_done, silu_now)
                for n, k in enumerate((0, 2, 1, 3) if last else range(KD)):
                    if last and k % 2:
                        pe.wait_ge(x1_lo_odd, k // 2 + 1)
                    else:
                        pe.wait_ge(x1_lo_done, c * KD + n + 1)
                    mm = three(bank[0][:], a_hi[:, k, :], a_lo[:, k, :], x1_hi[:, k, :], x1_lo[:, k, :],
                               n == 0, n == KD - 1)
                mm.then_inc(xa_done, 1)

            def h_base(m, psum, toks):
                cols = slice(m * P, (m + 1) * P)
                for k in range(KD):
                    three(psum, w_hi[:, k, cols], w_lo[:, k, cols], x1_hi[:, k, toks], x1_lo[:, k, toks],
                          k == 0, False)

            def h_adapt(c, m, psum, toks):
                cols = slice(m * P, (m + 1) * P)
                if m == 0:
                    pe.wait_ge(xa_lo_done, c + 1)
                three(psum, b_hi[:, cols], b_lo[:, cols], xa_hi[:, toks], xa_lo[:, toks], False, True
                      ).then_inc(h_done, 1)

            def ffn_tile(m, psum, toks, q_before):
                for k in range(KD):
                    if m == 0 and k % 2 == 0:
                        pe.wait_ge(q_done, q_before + k // 2 + 1)
                    mm = pe.matmul(psum, qw[:, k, m * P:(m + 1) * P], q[:, k, toks],
                                   start=(k == 0), stop=(k == KD - 1))
                mm.then_inc(ffn_done, 1)

            every = slice(0, TOK)

            def h_tile(c, m):
                h_base(m, bank[H_BANKS[m]][:], every)
                h_adapt(c, m, bank[H_BANKS[m]][:], every)

            def chunk(c, last, exact):
                n = c * TILES
                for i in range(TILES):
                    if i == H_AT:
                        adapter_down(c - 1, n + 1, False)
                        pe.wait_ge(hid_done, n + 1)
                        h_tile(c - 1, 0)
                        pe.wait_ge(silu_done, n + 2)
                        h_tile(c - 1, 1)
                        pe.wait_ge(hid_done, n + 2)
                        h_tile(c - 1, 2)
                        pe.wait_ge(h_out, (c - 1) * KD + 1)
                        h_tile(c - 1, 3)
                    if i == FFN_AT:
                        pe.wait_ge(qw_done, 1)
                        pe.wait_ge(hid_done, n + 6)
                        ffn_tile(0, bank[FFN_BANKS[0]][:], every, 2 * (c - 1))
                        ffn_tile(1, bank[FFN_BANKS[1]][:], every, 2 * (c - 1))
                        pe.wait_ge(silu_done, n + 7)
                        ffn_tile(2, bank[FFN_BANKS[2]][:], every, 2 * (c - 1))
                        pe.wait_ge(hid_done, n + 7)
                        ffn_tile(3, bank[FFN_BANKS[3]][:], every, 2 * (c - 1))
                    if i == 0:
                        pe.wait_ge(y_lo_done, (c + 1) * KD)
                    elif i == H_AT:
                        pe.wait_ge(xa_masked, c)
                    elif i == H_AT + 1:
                        pe.wait_ge(h_out, (c - 1) * KD + 2)
                    elif i == FFN_AT:
                        pe.wait_ge(deq_done, (c - 1) * KD + 1)
                    elif i == FFN_AT + 1:
                        pe.wait_ge(deq_done, (c - 1) * KD + 3)
                    elif i > 1:
                        pe.wait_ge(silu_done, n + i - 1)
                    a, b = gate_up(i, exact)
                    if i == H_AT:
                        pe.wait_ge(h_out, (c - 1) * KD + 4)
                    elif i == H_AT + 1:
                        pe.wait_ge(h_out, (c - 1) * KD + 3)
                    elif i == FFN_AT:
                        pe.wait_ge(deq_done, (c - 1) * KD + 2)
                    elif i == FFN_AT + 1:
                        pe.wait_ge(deq_done, (c - 1) * KD + 4)
                    elif i > 1:
                        pe.wait_ge(hid_done, n + i - 1)
                    up(i, b, exact)
                    if i == 1:
                        pe.wait_ge(x1_done, c * KD)
                    if i == TILES - 1 and not last:
                        mix(c + 1)
                    if i >= 1:
                        down(c, i - 1, exact)
                down(c, TILES - 1, exact)

            first_mix()
            for group in GROUPS:
                i0, i1 = group[0], group[-1]
                pe.wait_ge(flag_done, i1 + 1)
                low_bits = pe.value_load(flags[0:1, i1:i1 + 1].bitcast(I32))

                def tiles(exact):
                    for i in group:
                        if i == 0:
                            pe.wait_ge(y_lo_done, KD)
                        if i > 1:
                            pe.wait_ge(hid_done, i - 1)
                        if not exact:
                            pe.wait_ge(raw_in[i], 16)
                        a, b = gate_up(i, exact)
                        up(i, b, exact)
                        if i == TILES - 1:
                            mix(1)
                        if i >= 1:
                            down(0, i - 1, exact)
                    if i1 == TILES - 1:
                        down(0, TILES - 1, exact)
                with pe.If(low_bits == 0):
                    tiles(True)
                with pe.Else():
                    tiles(False)

            pe.wait_ge(w_lo_done, KD + 2)
            with pe.Fori(1, CHUNKS - 1) as c:
                with pe.If(low_bits == 0):
                    chunk(c, False, True)
                with pe.Else():
                    chunk(c, False, False)
            with pe.If(low_bits == 0):
                chunk(CHUNKS - 1, True, True)
            with pe.Else():
                chunk(CHUNKS - 1, True, False)

            c = CHUNKS - 1
            adapter_down(c, CHUNKS * TILES, True)
            for half in range(2):
                if half == 1:
                    pe.wait_ge(hid_done, CHUNKS * TILES)
                for m in range(KD):
                    h_base(m, last_bank(half, m), toks_of(half))
                for m in range(KD):
                    h_adapt(c, m, last_bank(half, m), toks_of(half))
            for half in range(2):
                pe.wait_ge(h_out, c * KD + (half + 1) * KD)
                for m in range(KD):
                    ffn_tile(m, last_bank(half, m), toks_of(half), 2 * (c + half))

        @block.scalar
        def _(act):
            act.wait_ge(mix_idx_in, 16)
            act.wait_ge(mixw_zero, 1)
            for j in range(NB // 2, NB):
                load_mix_weight(act, 0, j)
            def y_high(c):
                for t, b in enumerate(MIX_BANKS):
                    act.wait_ge(mix_done, c * KD + t + 1)
                    act.activation(y_hi[:, t, :], bank[b][:], ACT.Copy).then_inc(y_hi_done, 1)

            def silu(c, i, first):
                act.wait_ge(gate_done, c * TILES + i + 1)
                if not (first and i < 2):
                    act.wait_ge(hid_done, c * TILES + max(i - 1, 0))
                act.activation(gated[:, i % 2, :], bank[2 * (i % 2)][:], ACT.Silu,
                               scale=gs[:, i:i + 1]).then_inc(silu_done, 1)

            def hid_high(c, i, first):
                act.wait_ge(hid_done, c * TILES + i + 1)
                if i < 2 and not first:
                    act.wait_ge(acc_done, c * KD)
                elif i >= 2:
                    act.wait_ge(down_tile, c * (TILES - 1) + i - 1)
                act.activation(hid_hi[:, i % 2, :], hid[:, i % 2, :], ACT.Copy).then_inc(hid_hi_done, 1)

            def copy_h(n, m, psum, toks):
                act.wait_ge(h_done, n)
                act.activation(h[:, m, toks], psum, ACT.Copy).then_inc(h_out, 1)

            def keep_tile(i):
                act.wait_ge(tile_in[i], 16)
                act.activation(ffn0[:, i], tile_stage[i % STAGES], ACT.Copy).then_inc(tile_kept, 1)

            def x1_high(c):
                for m in range(KD):
                    act.wait_ge(x1_done, c * KD + m + 1)
                    act.activation(x1_hi[:, m, :], xc[:, m, :], ACT.Copy).then_inc(x1_hi_done, 1)

            def xa_high(c):
                act.wait_ge(xa_masked, c + 1)
                act.activation(xa_hi[:], xa[:], ACT.Copy).then_inc(xa_hi_done, 1)

            def chunk(c, last):
                for i in range(TILES):
                    if i == 0:
                        x1_high(c - 1)
                    if i == H_AT:
                        xa_high(c - 1)
                        for m in range(KD):
                            copy_h((c - 1) * KD + m + 1, m, bank[H_BANKS[m]][:], slice(0, TOK))
                    silu(c, i, False)
                    hid_high(c, i, False)
                if not last:
                    y_high(c + 1)

            act.wait_ge(warm_zero, 1)
            act.activation(silu_warm[:], silu_warm[:], ACT.Silu).then_inc(silu_ready, 1)
            keep_tile(0)
            y_high(0)
            keep_tile(1)
            act.wait_ge(small_in, 16 * 6)
            for i in range(TILES):
                silu(0, i, True)
                hid_high(0, i, True)
                for j in TEST_AFTER.get(i, ()):
                    keep_tile(j)
                if i == 4:
                    act.wait_ge(ab_in, 32)
                    act.activation(a_hi[:], a_stage[:], ACT.Copy).then_inc(w_hi_done, 1)
                if i == 5:
                    act.activation(b_hi[:], b_stage[:], ACT.Copy).then_inc(w_hi_done, 1)
                k = i - 7
                if 0 <= k < KD:
                    if k == 0:
                        act.wait_ge(w_in, 16)
                    act.activation(w_hi[:, k, :], w_stage[:, k, :], ACT.Copy).then_inc(w_hi_done, 1)
            y_high(1)
            with act.Fori(1, CHUNKS - 1) as c:
                chunk(c, False)
            chunk(CHUNKS - 1, True)
            x1_high(CHUNKS - 1)
            xa_high(CHUNKS - 1)
            for half in range(2):
                for m in range(KD):
                    copy_h((CHUNKS - 1 + half) * KD + m + 1, m, last_bank(half, m), toks_of(half))

        @block.vector
        def _(dve):
            def y_low(c):
                for t, b in enumerate(MIX_BANKS):
                    dve.wait_ge(y_hi_done, c * KD + t + 1)
                    dve.tensor_tensor(y_lo[:, t, :], bank[b][:], y_hi[:, t, :].bitcast(F32),
                                      ALU.subtract).then_inc(y_lo_done, 1)

            def hidden(c, i, first):
                dve.wait_ge(up_done, c * TILES + i + 1)
                dve.wait_ge(silu_done, c * TILES + i + 1)
                if not (first and i < 2):
                    dve.wait_ge(hid_lo_done, c * TILES + max(i - 1, 0))
                dve.scalar_tensor_tensor(out=hid[:, i % 2, :], in0=bank[2 * (i % 2) + 1][:], scalar=us[:, i:i + 1],
                                         in1=gated[:, i % 2, :], op0=ALU.mult, op1=ALU.mult
                                         ).then_inc(hid_done, 1)

            def x1(c):
                for m in range(KD):
                    dve.wait_ge(acc_done, c * KD + m + 1)
                    dve.wait_ge(xc_in[m], (c + 1) * 16)
                    dve.scalar_tensor_tensor(out=xc[:, m, :], in0=acc[m][:], scalar=ds[:, m:m + 1],
                                             in1=xc[:, m, :], op0=ALU.mult, op1=ALU.add).then_inc(x1_done, 1)

            def xa_mask(c):
                dve.wait_ge(xa_done, c + 1)
                of_batch = mask[:, bass.ds(c * NB, NB)].rearrange("p (b a) -> p b a", a=1).broadcast_to([P, NB, C])
                dve.tensor_tensor(xa[:].rearrange("p (b d) -> p b d", d=C),
                                  bank[0][:].rearrange("p (b d) -> p b d", d=C), of_batch,
                                  ALU.mult).then_inc(xa_masked, 1)

            every = slice(0, TOK)

            def h_max(n, toks):
                dve.wait_ge(h_out, (n + 1) * KD)
                dve.tensor_reduce(amax[:, toks], h[:, :, toks].rearrange("p m n -> p n m"), AX.X, ALU.max,
                                  apply_absolute_value=True).then_inc(amax_done, 1)

            def h_scale(n, toks):
                dve.wait_ge(amax_all_done, n + 1)
                dve.tensor_scalar(scale[:, toks], amax_all[:, toks], EPS, 1.0 / 127.0, ALU.max, ALU.mult
                                  ).then_inc(scale_done, 1)
                dve.wait_ge(scale_done, n + 1)
                dve.reciprocal(rscale[:, toks], scale[:, toks]).then_inc(rscale_done, 1)

            def quantise(n, pair, toks):
                ms = slice(2 * pair, 2 * pair + 2)
                step = 2 * n + pair + 1
                dve.wait_ge(rscale_done, n + 1)
                both = rscale[:, toks].rearrange("p (a n) -> p a n", a=1).broadcast_to([P, 2, toks.stop - toks.start])
                dve.tensor_tensor(h[:, ms, toks], h[:, ms, toks], both, ALU.mult).then_inc(q_scaled, 1)
                dve.wait_ge(q_scaled, step)
                dve.tensor_scalar(h[:, ms, toks], h[:, ms, toks], 127.0, -128.0, ALU.min, ALU.max
                                  ).then_inc(q_clipped, 1)
                dve.wait_ge(q_clipped, step)
                dve.tensor_scalar(q[:, ms, toks], h[:, ms, toks], ROUND, ROUND, ALU.add, ALU.subtract
                                  ).then_inc(q_done, 1)

            def result(n, m, psum, toks):
                dve.wait_ge(ffn_done, n * KD + m + 1)
                dve.scalar_tensor_tensor(out=deq[:, m % 2, toks], in0=psum, scalar=wsum[:, 2:3],
                                         in1=scale[:, toks], op0=ALU.mult, op1=ALU.mult).then_inc(deq_done, 1)
                dve.wait_ge(deq_done, n * KD + m + 1)
                dve.scalar_tensor_tensor(out=xc[:, m, toks], in0=deq[:, m % 2, toks], scalar=bs[:, m:m + 1],
                                         in1=xc[:, m, toks], op0=ALU.add, op1=ALU.add).then_inc(out_done, 1)

            def test_tile(i):
                low = tile_stage[i % STAGES].bitcast(I32)
                dve.wait_ge(tile_kept, i + 1)
                dve.tensor_scalar(low, low, LOW_BITS, None, ALU.bitwise_and).then_inc(low_done, 1)
                dve.wait_ge(low_done, i + 1)
                dve.tensor_reduce(inexact[:, i:i + 1], low, AX.XY, ALU.max).then_inc(inexact_done, 1)
                dve.wait_ge(inexact_done, i + 1)
                dve.tensor_reduce(inexact_to[:, i:i + 1], inexact[:, 0:i + 1], AX.X, ALU.max).then_inc(tested, 1)

            def chunk(c, last):
                x1(c - 1)
                for i in range(TILES):
                    if i == H_AT:
                        xa_mask(c - 1)
                        h_max(c - 1, every)
                    if i == FFN_AT:
                        for m in range(KD):
                            result(c - 1, m, bank[FFN_BANKS[m]][:], every)
                    hidden(c, i, False)
                    if i == SCALE_AFTER:
                        h_scale(c - 1, every)
                    for pair in range(2):
                        if i == Q_AFTER[pair]:
                            quantise(c - 1, pair, every)
                if not last:
                    y_low(c + 1)

            dve.memset(mixw[:], 0.0).then_inc(mixw_zero, 1)

            test_tile(0)
            y_low(0)
            test_tile(1)
            dve.wait_ge(iota_done, 2)
            dve.wait_ge(small_in, 16 * 6)
            dve.tensor_scalar(part_i[:, 1:2], part_i[:, 0:1], RANK.bit_length() - 1, None,
                              ALU.arith_shift_right).then_inc(mask_step, 1)
            dve.tensor_copy(nums[:], nums_i[:]).then_inc(mask_step, 1)
            dve.tensor_copy(ad_f[:], ad_i[:]).then_inc(mask_step, 1)
            dve.wait_ge(mask_step, 3)
            dve.tensor_copy(own_i[:], part_i[:, 1:2]).then_inc(mask_step, 1)
            dve.wait_ge(mask_step, 4)
            dve.scalar_tensor_tensor(out=own[:], in0=nums[:], scalar=own_i[:, 0:1], in1=scal[:],
                                     op0=ALU.is_equal, op1=ALU.mult).then_inc(mask_step, 1)
            dve.wait_ge(mask_step, 5)
            dve.tensor_reduce(own_s[:], own[:], AX.X, ALU.add).then_inc(mask_step, 1)
            dve.wait_ge(mask_step, 6)
            dve.tensor_scalar(mask[:], ad_f[:], own_i[:, 0:1], own_s[:, 0:1], ALU.is_equal, ALU.mult
                              ).then_inc(mask_step, 1)
            dve.wait_ge(mask_step, 7)

            for i in range(TILES):
                hidden(0, i, True)
                for j in TEST_AFTER.get(i, ()):
                    test_tile(j)
                if i == 8:
                    dve.wait_ge(qw_in, 16)
                    dve.tensor_reduce(wsum[:, 0:1], q_stage[:], AX.XY, ALU.add, apply_absolute_value=True
                                      ).then_inc(wsum_done, 1)
                if i == 9:
                    dve.wait_ge(wsum_all, 1)
                    dve.tensor_scalar(wsum[:, 2:3], wsum[:, 1:2], 1.0 / (D * D), EPS, ALU.mult, ALU.max
                                      ).then_inc(alpha_done, 1)
                    dve.wait_ge(alpha_done, 1)
                    dve.reciprocal(wsum[:, 3:4], wsum[:, 2:3]).then_inc(alpha_done, 1)
                    dve.wait_ge(alpha_done, 2)
                    dve.tensor_scalar(q_stage[:], q_stage[:], wsum[:, 3:4], 1.0, ALU.mult, ALU.min
                                      ).then_inc(qw_step, 1)
            y_low(1)
            dve.wait_ge(qw_step, 1)
            dve.tensor_scalar(q_stage[:], q_stage[:], -1.0, ROUND, ALU.max, ALU.add).then_inc(qw_step, 1)
            dve.wait_ge(qw_step, 2)
            dve.tensor_scalar(qw[:], q_stage[:], -ROUND, None, ALU.add).then_inc(qw_done, 1)

            with dve.Fori(1, CHUNKS - 1) as c:
                chunk(c, False)
            chunk(CHUNKS - 1, True)
            c = CHUNKS - 1
            x1(c)
            for m in (1, 3):
                dve.wait_ge(x1_hi_done, c * KD + m + 1)
                dve.tensor_tensor(x1_lo[:, m, :], xc[:, m, :], x1_hi[:, m, :].bitcast(F32),
                                  ALU.subtract).then_inc(x1_lo_odd, 1)
            xa_mask(c)
            for half in range(2):
                n, toks = c + half, toks_of(half)
                h_max(n, toks)
                if half == 1:
                    result(c, 0, last_bank(0, 0), toks_of(0))
                    result(c, 1, last_bank(0, 1), toks_of(0))
                h_scale(n, toks)
                quantise(n, 0, toks)
                quantise(n, 1, toks)
            for half, m in ((0, 2), (0, 3), (1, 0), (1, 1), (1, 2), (1, 3)):
                result(c + half, m, last_bank(half, m), toks_of(half))

        @block.gpsimd
        def _(pool):
            def hid_low(c, i, first):
                pool.wait_ge(hid_hi_done, c * TILES + i + 1)
                pool.tensor_tensor(hid_lo[:, i % 2, :], hid[:, i % 2, :], hid_hi[:, i % 2, :].bitcast(F32),
                                   ALU.subtract).then_inc(hid_lo_done, 1)

            def x1_low(c, ms):
                for m in ms:
                    pool.wait_ge(x1_hi_done, c * KD + m + 1)
                    pool.tensor_tensor(x1_lo[:, m, :], xc[:, m, :], x1_hi[:, m, :].bitcast(F32),
                                       ALU.subtract).then_inc(x1_lo_done, 1)

            def xa_low(c):
                pool.wait_ge(xa_hi_done, c + 1)
                pool.tensor_tensor(xa_lo[:], xa[:], xa_hi[:].bitcast(F32), ALU.subtract).then_inc(xa_lo_done, 1)

            def max_all(n, toks):
                pool.wait_ge(wsum_all, 1)
                pool.wait_ge(amax_done, n + 1)
                pool.partition_all_reduce(amax_all[:, toks], amax[:, toks], P, RMAX).then_inc(amax_all_done, 1)

            def flag(i):
                pool.wait_ge(tested, i + 1)
                pool.partition_all_reduce(flags[:, i:i + 1], inexact_to[:, i:i + 1], P, RMAX).then_inc(flag_done, 1)

            def chunk(c):
                x1_low(c - 1, range(KD - 1))
                for i in range(TILES):
                    if i == 1:
                        x1_low(c - 1, (KD - 1,))
                    if i == H_AT:
                        xa_low(c - 1)
                        max_all(c - 1, slice(0, TOK))
                    hid_low(c, i, False)

            pool.memset(silu_warm[:], 0.0).then_inc(warm_zero, 1)
            for dst, src in ((gs[:], gate_s), (us[:], up_s), (ds[:], down_s), (bs[:], bias)):
                pool.dma_start(dst, src).then_inc(small_in, 16)
            pool.dma_start(ad_i[:], adapter_idx.rearrange("(a b) -> a b", a=1).broadcast_to([P, BATCHES])
                          ).then_inc(small_in, 16)
            pool.dma_start(scal[:], scalings.rearrange("(a b) -> a b", a=1).broadcast_to([P, P // RANK])
                          ).then_inc(small_in, 16)
            pool.dma_start(a_stage[:], a_t).then_inc(ab_in, 16)
            pool.dma_start(b_stage[:], b_t).then_inc(ab_in, 16)
            pool.iota(part_i[:, 0:1], pattern=[[0, 1]], base=0, channel_multiplier=1).then_inc(iota_done, 1)
            pool.iota(nums_i[:], pattern=[[1, P // RANK]], base=0, channel_multiplier=0).then_inc(iota_done, 1)
            flag(0)
            flag(1)
            for i in range(TILES):
                hid_low(0, i, True)
                for j in TEST_AFTER.get(i, ()):
                    flag(j)
                if i == 8:
                    pool.wait_ge(wsum_done, 1)
                    pool.partition_all_reduce(wsum[:, 1:2], wsum[:, 0:1], P, RADD).then_inc(wsum_all, 1)
                if i == 5:
                    pool.wait_ge(w_hi_done, 1)
                    pool.tensor_tensor(a_lo[:], a_stage[:], a_hi[:].bitcast(F32), ALU.subtract).then_inc(w_lo_done, 1)
                if i == 6:
                    pool.wait_ge(w_hi_done, 2)
                    pool.tensor_tensor(b_lo[:], b_stage[:], b_hi[:].bitcast(F32), ALU.subtract).then_inc(w_lo_done, 1)
                k = i - 7
                if 0 <= k < KD:
                    pool.wait_ge(w_hi_done, 2 + k + 1)
                    pool.tensor_tensor(w_lo[:, k, :], w_stage[:, k, :], w_hi[:, k, :].bitcast(F32),
                                       ALU.subtract).then_inc(w_lo_done, 1)
            with pool.Fori(1, CHUNKS) as c:
                chunk(c)
            x1_low(CHUNKS - 1, (0, 2))
            xa_low(CHUNKS - 1)
            for half in range(2):
                max_all(CHUNKS - 1 + half, toks_of(half))


def kernel(x, itok_B_1_198, itok_B_0_6, L0_cond_weights, L0_ffn_gate_w, L0_ffn_up_w, L0_ffn_down_w, L0_ffn_gate_s,
           L0_ffn_up_s, L0_ffn_down_s, L1_cond_W, L1_cond_A, L1_cond_Bm, L1_cond_scalings, L1_ffn_weight, L1_ffn_bias):
    import numpy as np
    import concourse.bacc as bacc
    from concourse.bass_utils import run_bass_kernel_spmd

    a = np.asarray
    batches, chans, d = x.shape
    kd, tiles = d // P, L0_ffn_gate_w.shape[0] // P

    def rows_in(w):
        return a(w).T.reshape(kd, P, -1).transpose(1, 0, 2)

    def by_tile(w):
        return a(w).reshape(tiles, P, kd, P).transpose(3, 0, 2, 1).reshape(P, tiles, d)

    down = a(L0_ffn_down_w).reshape(kd, P, tiles, P).transpose(3, 2, 0, 1).reshape(P, tiles, d)
    ins = {
        "x_rows": a(x),
        "x_cols": a(x).transpose(2, 0, 1).reshape(d, batches * chans),
        "mix_idx": a(itok_B_1_198),
        "adapter_idx": a(itok_B_0_6),
        "mix_w": a(L0_cond_weights),
        "ffn0_w": np.stack([by_tile(L0_ffn_gate_w), by_tile(L0_ffn_up_w), down], axis=2),
        "gate_s": a(L0_ffn_gate_s).reshape(tiles, P).T,
        "up_s": a(L0_ffn_up_s).reshape(tiles, P).T,
        "down_s": a(L0_ffn_down_s).reshape(kd, P).T,
        "w_t": rows_in(L1_cond_W),
        "a_t": rows_in(a(L1_cond_A).reshape(P, d)),
        "b_t": a(L1_cond_Bm).transpose(0, 2, 1).reshape(P, d),
        "scalings": a(L1_cond_scalings),
        "qw_t": rows_in(L1_ffn_weight),
        "bias": a(L1_ffn_bias).reshape(kd, P).T,
    }
    nc = bacc.Bacc("TRN2", target_bir_lowering=False, num_devices=1)
    arrays, args = {}, []
    for name, v in ins.items():
        v = np.ascontiguousarray(v)
        arrays[name] = v
        args.append(nc.dram_tensor(name, v.shape, mybir.dt.from_np(v.dtype), kind="ExternalInput").ap())
    args.append(nc.dram_tensor("out", (d, batches * chans), F32, kind="ExternalOutput").ap())
    adaln_ffn_kernel(nc, *args)
    r = run_bass_kernel_spmd(nc, [arrays], core_ids=[0])
    return r.results[0]["out"].reshape(d, batches, chans).transpose(1, 2, 0)
```

```python
from contextlib import ExitStack

import concourse.bass as bass
from concourse import mybir

ALU = mybir.AluOpType
ACT = mybir.ActivationFunctionType
AX = mybir.AxisListType
F32 = mybir.dt.float32
F32R = mybir.dt.float32r
BF16 = mybir.dt.bfloat16
I32 = mybir.dt.int32
RMAX = bass.bass_isa.ReduceOp.max
RADD = bass.bass_isa.ReduceOp.add

P = 128
LOW_BITS = 0xFFF
ROUND = 12582912.0
EPS = 1e-5


def adaln_ffn_kernel(nc, x_rows, x_cols, mix_idx, adapter_idx, mix_w, ffn0_w, vectors,
                     w_t, a_t, b_t, scalings, qw_t, out):
    BATCHES, C, D = x_rows.shape
    N_MIX = mix_w.shape[0]
    TILES = ffn0_w.shape[1]
    KD = D // P
    TOK = 512
    NB = TOK // C
    PAIRS = NB // 2
    CHUNKS = BATCHES // NB
    RANK = P // scalings.shape[0]
    H_AT, FFN_AT = 2, 7
    SCALE_AFTER, Q_AFTER = 3, (3, 4)
    GROUPS = ((0,), (1,), (2,), (3, 4), (5, 6), (7, 8), (9, 10))
    TEST_AFTER = {i: (i + 3,) for i in range(TILES - 3)}
    BLOCKS = (slice(0, 192), slice(192, 384), slice(384, 512))
    RESULTS = (slice(0, 384), slice(384, 512))
    POOL_TILES = 2
    SP_MIX, ACT_MIX = (0, 2, 4, 6, 7), (1, 3, 5)
    WARM = 16
    MIX_BANKS = (2, 3, 0, 1)
    H_BANKS = (1, 2, 3, 1)
    FFN_BANKS = (2, 3, 0, 1)

    with ExitStack() as ctx:
        def sb(name, shape, dt):
            return ctx.enter_context(nc.sbuf_tensor(name, shape, dt))

        def sem(name):
            return ctx.enter_context(nc.semaphore(name))

        ffn0 = sb("ffn0", [P, TILES, 3, D], F32R)
        w_hi = sb("w_hi", [P, KD, D], F32R)
        w_lo = sb("w_lo", [P, KD, D], F32R)
        a_hi = sb("a_hi", [P, KD, P], F32R)
        a_lo = sb("a_lo", [P, KD, P], F32R)
        b_hi = sb("b_hi", [P, D], F32R)
        b_lo = sb("b_lo", [P, D], F32R)
        qw = sb("qw", [P, KD, D], BF16)
        w_stage = sb("w_stage", [P, KD, D], F32)
        a_stage = sb("a_stage", [P, KD, P], F32)
        b_stage = sb("b_stage", [P, D], F32)

        xr = sb("xr", [P, PAIRS, D], F32)
        mixw = sb("mixw", [P, PAIRS, P], F32)
        y_hi = sb("y_hi", [P, KD, TOK], F32R)
        y_lo = sb("y_lo", [P, KD, TOK], F32R)
        gated = sb("gated", [P, 2, TOK], F32)
        hid = sb("hid", [P, 2, TOK], F32)
        hid_hi = sb("hid_hi", [P, 2, TOK], F32R)
        hid_lo = sb("hid_lo", [P, 2, TOK], F32R)
        xc = sb("xc", [P, KD, TOK], F32)
        x1_hi = sb("x1_hi", [P, KD, TOK], F32R)
        x1_lo = sb("x1_lo", [P, KD, TOK], F32R)
        xa = sb("xa", [P, TOK], F32)
        xa_hi = sb("xa_hi", [P, TOK], F32R)
        xa_lo = sb("xa_lo", [P, TOK], F32R)
        h = sb("h", [P, KD, TOK], F32)
        per_token = sb("per_token", [P, 4, TOK], F32)
        amax = per_token[:, 0, :]
        amax_all = per_token[:, 1, :]
        scale = per_token[:, 2, :]
        rscale = per_token[:, 3, :]
        q_stage = per_token
        q = sb("q", [P, KD, TOK], BF16)
        deq = sb("deq", [P, 2, TOK], F32)

        vecs = sb("vecs", [P, 2 * TILES + 2 * KD], F32)
        gs = vecs[:, 0:TILES]
        us = vecs[:, TILES:2 * TILES]
        ds = vecs[:, 2 * TILES:2 * TILES + KD]
        bs = vecs[:, 2 * TILES + KD:]
        mix_i = sb("mix_i", [1, BATCHES], I32)
        ad_i = sb("ad_i", [P, BATCHES], I32)
        ad_f = sb("ad_f", [P, BATCHES], F32)
        scal = sb("scal", [P, P // RANK], F32)
        part_i = sb("part_i", [P, 2], I32)
        nums_i = sb("nums_i", [P, P // RANK], I32)
        own_i = sb("own_i", [P, 1], F32)
        nums = sb("nums", [P, P // RANK], F32)
        own = sb("own", [P, P // RANK], F32)
        own_s = sb("own_s", [P, 1], F32)
        mask = sb("mask", [P, BATCHES], F32)
        inexact = sb("inexact", [P, TILES], F32)
        inexact_to = sb("inexact_to", [P, TILES], F32)
        flags = sb("flags", [P, TILES], F32)
        tile_stage = [h[:, 0:3, :], xc[:, 0:3, :], w_stage[:, 0:3, :]]
        STAGES = len(tile_stage)
        raw = nc.dram_tensor("raw", (P, TILES, 3, D), F32).ap()
        pe_warm = sb("pe_warm", [P, TOK], BF16)
        silu_warm = sb("silu_warm", [P, 1], F32)
        wsum = sb("wsum", [P, 4], F32)

        bank = [ctx.enter_context(nc.psum_tensor(f"bank{n}", [P, TOK], F32)) for n in range(4)]
        acc = [ctx.enter_context(nc.psum_tensor(f"acc{m}", [P, TOK], F32)) for m in range(KD)]

        mix_psum = [bank[b] for b in MIX_BANKS]

        small_in = sem("small_in")
        mix_idx_in = sem("mix_idx_in")
        ab_in = sem("ab_in")
        w_in = sem("w_in")
        qw_in = sem("qw_in")
        tile_in = [sem(f"tile_in{i}") for i in range(TILES)]
        raw_copied = [sem(f"raw_copied{i}") for i in range(TILES)]
        raw_in = [sem(f"raw_in{i}") for i in range(TILES)]
        xr_in = sem("xr_in")
        mixw_in = [sem(f"mixw_in{pair}") for pair in range(PAIRS)]
        xc_in = [sem(f"xc_in{m}") for m in range(KD)]
        stored = [sem(f"stored{m}") for m in range(KD)]
        mix_done = sem("mix_done")
        gate_done = sem("gate_done")
        up_done = sem("up_done")
        down_tile = sem("down_tile")
        acc_done = sem("acc_done")
        xa_done = sem("xa_done")
        h_done = sem("h_done")
        ffn_done = sem("ffn_done")
        y_hi_done = sem("y_hi_done")
        silu_done = sem("silu_done")
        hid_hi_done = sem("hid_hi_done")
        x1_hi_done = sem("x1_hi_done")
        xa_hi_done = sem("xa_hi_done")
        h_out = sem("h_out")
        tile_kept = sem("tile_kept")
        silu_ready = sem("silu_ready")
        w_hi_done = sem("w_hi_done")
        mixw_zero = sem("mixw_zero")
        mask_step = sem("mask_step")
        low_done = sem("low_done")
        inexact_done = sem("inexact_done")
        tested = sem("tested")
        y_lo_done = sem("y_lo_done")
        hid_done = sem("hid_done")
        x1_done = sem("x1_done")
        x1_lo_odd = sem("x1_lo_odd")
        xa_masked = sem("xa_masked")
        amax_done = sem("amax_done")
        scale_done = sem("scale_done")
        rscale_done = sem("rscale_done")
        q_scaled = sem("q_scaled")
        q_clipped = sem("q_clipped")
        q_done = sem("q_done")
        deq_done = sem("deq_done")
        out_done = sem("out_done")
        wsum_done = sem("wsum_done")
        alpha_done = sem("alpha_done")
        qw_step = sem("qw_step")
        qw_done = sem("qw_done")
        warm_zero = sem("warm_zero")
        iota_done = sem("iota_done")
        flag_done = sem("flag_done")
        hid_lo_done = sem("hid_lo_done")
        x1_lo_done = sem("x1_lo_done")
        xa_lo_done = sem("xa_lo_done")
        amax_all_done = sem("amax_all_done")
        pool_out = sem("pool_out")
        hid_lo_last = sem("hid_lo_last")
        bias_added = sem("bias_added")
        w_lo_done = sem("w_lo_done")
        wsum_all = sem("wsum_all")

        xr_dram = x_rows.rearrange("(g q b) c t -> g (b c) q t", q=PAIRS, b=2)
        mix_idx_dram = mix_idx.rearrange("(a b) -> a b", a=1)

        def tok(c):
            return bass.ds(c * TOK, TOK)

        bank_sets = ([acc[0], bank[1], bank[2], bank[3]], [bank[0], acc[1], acc[2], acc[3]])
        H_SET = (0, 1, 0)
        FFN_SET = (1, 1, 0)

        def h_psum(n, m):
            return bank_sets[H_SET[n]][m][:, BLOCKS[n]]

        def ffn_psum(n, m):
            return bank_sets[FFN_SET[n]][m][:, BLOCKS[n]]

        def load_mix_weight(eng, c, j):
            w = eng.value_load(mix_i[0:1, bass.ds(c * NB + j, 1)], min_val=0, max_val=N_MIX - 1)
            half = slice(C * (j % 2), C * (j % 2) + C)
            eng.dma_start(mixw[half, j // 2, half],
                          mix_w[bass.ds(w, 1)].rearrange("a c d -> (a c) d")).then_inc(mixw_in[j // 2], 16)

        block = ctx.enter_context(nc.Block())

        @block.sync
        def _(sp):
            def load_rows(c):
                sp.dma_start(xr[:], xr_dram[bass.ds(c, 1)].rearrange("a p q t -> (a p) q t")).then_inc(xr_in, 16)

            def load_mix(c):
                load_rows(c)
                for j in range(NB):
                    load_mix_weight(sp, c, j)

            def load_cols(c, m):
                sp.dma_start(xc[:, m, :], x_cols[m * P:(m + 1) * P, tok(c)]).then_inc(xc_in[m], 16)

            def store(c):
                for m in range(KD):
                    sp.wait_ge(out_done, KD * c + m + 1)
                    sp.dma_start(out[m * P:(m + 1) * P, tok(c)], xc[:, m, :]).then_inc(stored[m], 16)

            def load_tile(i):
                if i >= STAGES:
                    sp.wait_ge(tested, i - STAGES + 1)
                sp.dma_start(tile_stage[i % STAGES], ffn0_w[:, i]
                             ).then_inc(tile_in[i], 16)

            def load_raw(group):
                sp.wait_ge(flag_done, group[-1] + 1)
                low_bits = sp.value_load(flags[0:1, group[-1]:group[-1] + 1].bitcast(I32))
                with sp.If(low_bits != 0):
                    for i in group:
                        sp.dma_start(raw[:, i], ffn0_w[:, i]).then_inc(raw_copied[i], 16)
                    for i in group:
                        sp.wait_ge(raw_copied[i], 16)
                        sp.dma_start(ffn0[:, i].bitcast(F32), raw[:, i]).then_inc(raw_in[i], 16)
                with sp.Else():
                    sp.nop()

            sp.dma_start(mix_i[:], mix_idx_dram).then_inc(mix_idx_in, 16)
            load_tile(0)
            load_rows(0)
            sp.wait_ge(mix_idx_in, 16)
            sp.wait_ge(mixw_zero, 1)
            for j in SP_MIX:
                load_mix_weight(sp, 0, j)
            load_tile(1)
            load_tile(2)
            for i in range(STAGES, TILES):
                load_tile(i)
                if i == TILES // 2:
                    sp.dma_start(q_stage[:], qw_t).then_inc(qw_in, 16)
                for group in GROUPS:
                    if group[-1] == i - STAGES:
                        load_raw(group)
            sp.wait_ge(tested, TILES - 2)
            sp.dma_start(w_stage[:], w_t).then_inc(w_in, 16)
            sp.wait_ge(mix_done, KD)
            load_mix(1)
            for group in GROUPS:
                if TILES - STAGES <= group[-1] < TILES - 1:
                    load_raw(group)
            sp.wait_ge(tested, TILES)
            for m in range(KD):
                load_cols(0, m)
            load_raw(GROUPS[-1])

            def steady(c, last):
                if not last:
                    sp.wait_ge(mix_done, (c + 1) * KD)
                    load_mix(c + 1)
                store(c - 1)
                for m in range(KD):
                    sp.wait_ge(stored[m], c * 16)
                    load_cols(c, m)

            with sp.Fori(1, CHUNKS - 1) as c:
                steady(c, False)
            steady(CHUNKS - 1, True)
            c = CHUNKS - 1
            for n, toks in enumerate(RESULTS):
                for m in range(KD):
                    if n == 0 and m < POOL_TILES:
                        sp.wait_ge(pool_out, m + 1)
                    else:
                        sp.wait_ge(out_done, (c + n) * KD + m + 1 - POOL_TILES)
                    sp.dma_start(out[m * P:(m + 1) * P, c * TOK + toks.start:c * TOK + toks.stop],
                                 xc[:, m, toks]).then_inc(stored[m], 16)
            for m in range(KD):
                sp.wait_ge(stored[m], (c + len(RESULTS)) * 16)

        @block.tensor
        def _(pe):
            def mix_product(psum, t, pair):
                return pe.matmul(psum[t][:, pair * P:(pair + 1) * P], xr[:, pair, t * P:(t + 1) * P],
                                 mixw[:, pair, :], start=True, stop=True)

            def first_mix():
                pe.wait_ge(xr_in, 16)
                for pair in range(PAIRS):
                    pe.wait_ge(mixw_in[pair], 2 * 16)
                    for t in range(KD):
                        mm = mix_product(acc, t, pair)
                        if pair == PAIRS - 1:
                            mm.then_inc(mix_done, 1)

            def mix(c):
                pe.wait_ge(xr_in, (c + 1) * 16)
                for pair in range(PAIRS):
                    pe.wait_ge(mixw_in[pair], (c + 1) * 2 * 16)
                for t in range(KD):
                    if t == 0:
                        pe.wait_ge(hid_done, c * TILES - 1)
                    if t == 2:
                        pe.wait_ge(silu_done, c * TILES)
                    if t == 3:
                        pe.wait_ge(hid_done, c * TILES)
                    for pair in range(PAIRS):
                        mm = mix_product(mix_psum, t, pair)
                    mm.then_inc(mix_done, 1)

            def split_products(psum, lhs, hi, lo, exact, first, last, ready=None):
                n = len(lhs)
                for k in range(n):
                    if ready is not None:
                        pe.wait_ge(ready, k + 1)
                    for part in (hi[k], lo[k]):
                        mm = pe.matmul(psum, lhs[k][exact], part if exact else part.bitcast(F32),
                                       start=first and k == 0 and part is hi[k],
                                       stop=last and k == n - 1 and part is lo[k])
                return mm

            def weight(i, which, k):
                w = ffn0[:, i, which, k * P:(k + 1) * P]
                return w.bitcast(F32), w

            ys_hi = [y_hi[:, k, :] for k in range(KD)]
            ys_lo = [y_lo[:, k, :] for k in range(KD)]

            def gate(i, exact, ready=None):
                a, b = 2 * (i % 2), 2 * (i % 2) + 1
                split_products(bank[a][:], [weight(i, 0, k) for k in range(KD)], ys_hi, ys_lo, exact,
                               True, True, ready).then_inc(gate_done, 1)
                return a, b

            def up(i, b, exact):
                split_products(bank[b][:], [weight(i, 1, k) for k in range(KD)], ys_hi, ys_lo, exact,
                               True, True).then_inc(up_done, 1)

            def down(c, i, exact):
                pe.wait_ge(hid_lo_done, c * TILES + i + 1)
                for m in range(KD):
                    mm = split_products(acc[m][:], [weight(i, 2, m)], [hid_hi[:, i % 2, :]], [hid_lo[:, i % 2, :]],
                                        exact, i == 0, i == TILES - 1)
                    if i == TILES - 1:
                        mm.then_inc(acc_done, 1)
                if i < TILES - 1:
                    mm.then_inc(down_tile, 1)

            def three(psum, whi, wlo, hi, lo, first, last):
                pe.matmul(psum, whi, hi, start=first, stop=False)
                pe.matmul(psum, whi, lo, start=False, stop=False)
                return pe.matmul(psum, wlo, hi, start=False, stop=last)

            def adapter_down(c):
                for k in range(KD):
                    pe.wait_ge(x1_lo_done, c * KD + k + 1)
                    mm = three(bank[0][:], a_hi[:, k, :], a_lo[:, k, :], x1_hi[:, k, :], x1_lo[:, k, :],
                               k == 0, k == KD - 1)
                mm.then_inc(xa_done, 1)

            def h_base(m, psum, toks):
                cols = slice(m * P, (m + 1) * P)
                for k in range(KD):
                    three(psum, w_hi[:, k, cols], w_lo[:, k, cols], x1_hi[:, k, toks], x1_lo[:, k, toks],
                          k == 0, False)

            def h_adapt(c, m, psum, toks):
                cols = slice(m * P, (m + 1) * P)
                if m == 0:
                    pe.wait_ge(xa_lo_done, c + 1)
                three(psum, b_hi[:, cols], b_lo[:, cols], xa_hi[:, toks], xa_lo[:, toks], False, True
                      ).then_inc(h_done, 1)

            def ffn_tile(m, psum, toks, q_before):
                for k in range(KD):
                    if m == 0 and k % 2 == 0:
                        pe.wait_ge(q_done, q_before + k // 2 + 1)
                    mm = pe.matmul(psum, qw[:, k, m * P:(m + 1) * P], q[:, k, toks],
                                   start=(k == 0), stop=(k == KD - 1))
                mm.then_inc(ffn_done, 1)

            every = slice(0, TOK)

            def h_tile(c, m):
                h_base(m, bank[H_BANKS[m]][:], every)
                h_adapt(c, m, bank[H_BANKS[m]][:], every)

            def chunk(c, last, exact):
                n = c * TILES
                for i in range(TILES):
                    if i == H_AT:
                        pe.wait_ge(silu_done, n + 1)
                        adapter_down(c - 1)
                        pe.wait_ge(hid_done, n + 1)
                        h_base(0, bank[H_BANKS[0]][:], every)
                        pe.wait_ge(silu_done, n + 2)
                        h_base(1, bank[H_BANKS[1]][:], every)
                        h_adapt(c - 1, 0, bank[H_BANKS[0]][:], every)
                        h_adapt(c - 1, 1, bank[H_BANKS[1]][:], every)
                        pe.wait_ge(hid_done, n + 2)
                        h_tile(c - 1, 2)
                        pe.wait_ge(h_out, (c - 1) * KD + 1)
                        h_tile(c - 1, 3)
                    if i == FFN_AT:
                        pe.wait_ge(qw_done, 1)
                        pe.wait_ge(hid_done, n + 6)
                        ffn_tile(0, bank[FFN_BANKS[0]][:], every, 2 * (c - 1))
                        ffn_tile(1, bank[FFN_BANKS[1]][:], every, 2 * (c - 1))
                        pe.wait_ge(silu_done, n + 7)
                        ffn_tile(2, bank[FFN_BANKS[2]][:], every, 2 * (c - 1))
                        pe.wait_ge(hid_done, n + 7)
                        ffn_tile(3, bank[FFN_BANKS[3]][:], every, 2 * (c - 1))
                    if i == 0:
                        pe.wait_ge(y_lo_done, (c + 1) * KD)
                    elif i == H_AT:
                        pe.wait_ge(xa_masked, c)
                    elif i == H_AT + 1:
                        pe.wait_ge(h_out, (c - 1) * KD + 2)
                    elif i == FFN_AT:
                        pe.wait_ge(deq_done, (c - 1) * KD + 1)
                    elif i == FFN_AT + 1:
                        pe.wait_ge(deq_done, (c - 1) * KD + 3)
                    elif i > 1:
                        pe.wait_ge(silu_done, n + i - 1)
                    a, b = gate(i, exact)
                    if i == H_AT:
                        pe.wait_ge(h_out, (c - 1) * KD + 4)
                    elif i == H_AT + 1:
                        pe.wait_ge(h_out, (c - 1) * KD + 3)
                    elif i == FFN_AT:
                        pe.wait_ge(deq_done, (c - 1) * KD + 2)
                    elif i == FFN_AT + 1:
                        pe.wait_ge(deq_done, (c - 1) * KD + 4)
                    elif i > 1:
                        pe.wait_ge(hid_done, n + i - 1)
                    up(i, b, exact)
                    if i == 1:
                        pe.wait_ge(x1_done, c * KD)
                    if i == TILES - 1 and not last:
                        mix(c + 1)
                    if i >= 1:
                        down(c, i - 1, exact)
                if not last:
                    down(c, TILES - 1, exact)
                    return
                for ready, part in ((hid_hi_done, hid_hi), (hid_lo_last, hid_lo)):
                    pe.wait_ge(ready, CHUNKS * TILES if ready is hid_hi_done else 1)
                    moving = part[:, (TILES - 1) % 2, :]
                    for m in range(KD):
                        mm = pe.matmul(acc[m][:], weight(TILES - 1, 2, m)[exact],
                                       moving if exact else moving.bitcast(F32),
                                       start=False, stop=part is hid_lo)
                        if part is hid_lo:
                            mm.then_inc(acc_done, 1)

            pe.wait_ge(warm_zero, 2)
            for _ in range(WARM):
                pe.matmul(bank[0][:], pe_warm[:, 0:P], pe_warm[:], start=True, stop=True)

            first_mix()
            for group in GROUPS:
                i0, i1 = group[0], group[-1]
                pe.wait_ge(flag_done, i1 + 1)
                low_bits = pe.value_load(flags[0:1, i1:i1 + 1].bitcast(I32))

                def tiles(exact):
                    for i in group:
                        if i > 1:
                            pe.wait_ge(hid_done, i - 1)
                        if not exact:
                            pe.wait_ge(raw_in[i], 16)
                        a, b = gate(i, exact, y_lo_done if i == 0 else None)
                        up(i, b, exact)
                        if i == TILES - 1:
                            mix(1)
                        if i >= 1:
                            down(0, i - 1, exact)
                    if i1 == TILES - 1:
                        down(0, TILES - 1, exact)
                with pe.If(low_bits == 0):
                    tiles(True)
                with pe.Else():
                    tiles(False)

            pe.wait_ge(w_lo_done, KD + 2)
            with pe.Fori(1, CHUNKS - 1) as c:
                with pe.If(low_bits == 0):
                    chunk(c, False, True)
                with pe.Else():
                    chunk(c, False, False)
            with pe.If(low_bits == 0):
                chunk(CHUNKS - 1, True, True)
            with pe.Else():
                chunk(CHUNKS - 1, True, False)

            c = CHUNKS - 1
            blk = BLOCKS[0]
            pe.wait_ge(silu_done, CHUNKS * TILES)
            pe.wait_ge(hid_done, CHUNKS * TILES)
            for k in range(KD):
                pe.wait_ge(x1_hi_done, c * KD + k + 1)
                for a in (a_hi, a_lo):
                    pe.matmul(bank[0][:], a[:, k, :], x1_hi[:, k, :], start=(k == 0 and a is a_hi), stop=False)
                for m in range(KD):
                    for w in (w_hi, w_lo):
                        pe.matmul(h_psum(0, m), w[:, k, m * P:(m + 1) * P], x1_hi[:, k, blk],
                                  start=(k == 0 and w is w_hi), stop=False)
            for k in range(KD):
                if k % 2:
                    pe.wait_ge(x1_lo_odd, k // 2 + 1)
                else:
                    pe.wait_ge(x1_lo_done, c * KD + k // 2 + 1)
                mm = pe.matmul(bank[0][:], a_hi[:, k, :], x1_lo[:, k, :], start=False, stop=(k == KD - 1))
            mm.then_inc(xa_done, 1)
            for m in range(KD):
                for k in range(KD):
                    pe.matmul(h_psum(0, m), w_hi[:, k, m * P:(m + 1) * P], x1_lo[:, k, blk],
                              start=False, stop=False)
            h_base(1, h_psum(1, 1), BLOCKS[1])
            h_base(2, h_psum(1, 2), BLOCKS[1])
            for m in range(KD):
                h_adapt(c, m, h_psum(0, m), BLOCKS[0])
            h_base(3, h_psum(1, 3), BLOCKS[1])
            pe.wait_ge(xa_masked, CHUNKS)
            h_base(0, h_psum(1, 0), BLOCKS[1])
            for m in range(KD):
                h_adapt(c, m, h_psum(1, m), BLOCKS[1])
            for m in range(KD):
                pe.wait_ge(h_out, c * KD + m + 1)
                h_base(m, h_psum(2, m), BLOCKS[2])
            for m in range(KD):
                h_adapt(c, m, h_psum(2, m), BLOCKS[2])
            pe.wait_ge(h_out, (c + len(BLOCKS)) * KD)
            for n, toks in enumerate(BLOCKS):
                for m in range(KD):
                    ffn_tile(m, ffn_psum(n, m), toks, 2 * (c + n))

        @block.scalar
        def _(act):
            act.wait_ge(warm_zero, 1)
            act.activation(silu_warm[:], silu_warm[:], ACT.Silu).then_inc(silu_ready, 1)

            def y_high(c, psum):
                for t in range(KD):
                    act.wait_ge(mix_done, c * KD + t + 1)
                    act.activation(y_hi[:, t, :], psum[t][:], ACT.Copy).then_inc(y_hi_done, 1)

            def silu(c, i, first):
                act.wait_ge(gate_done, c * TILES + i + 1)
                if not (first and i < 2):
                    act.wait_ge(hid_done, c * TILES + max(i - 1, 0))
                act.activation(gated[:, i % 2, :], bank[2 * (i % 2)][:], ACT.Silu,
                               scale=gs[:, i:i + 1]).then_inc(silu_done, 1)

            def hid_high(c, i, first):
                act.wait_ge(hid_done, c * TILES + i + 1)
                if i < 2 and not first:
                    act.wait_ge(acc_done, c * KD)
                elif i >= 2:
                    act.wait_ge(down_tile, c * (TILES - 1) + i - 1)
                act.activation(hid_hi[:, i % 2, :], hid[:, i % 2, :], ACT.Copy).then_inc(hid_hi_done, 1)

            def copy_h(n, m, psum, toks):
                act.wait_ge(h_done, n)
                act.activation(h[:, m, toks], psum, ACT.Copy).then_inc(h_out, 1)

            def keep_tile(i):
                act.wait_ge(tile_in[i], 16)
                act.activation(ffn0[:, i], tile_stage[i % STAGES], ACT.Copy).then_inc(tile_kept, 1)

            def x1_high(c):
                for m in range(KD):
                    act.wait_ge(x1_done, c * KD + m + 1)
                    act.activation(x1_hi[:, m, :], xc[:, m, :], ACT.Copy).then_inc(x1_hi_done, 1)

            def xa_high(c):
                act.wait_ge(xa_masked, c + 1)
                act.activation(xa_hi[:], xa[:], ACT.Copy).then_inc(xa_hi_done, 1)

            def chunk(c, last):
                for i in range(TILES):
                    if i == 0:
                        x1_high(c - 1)
                    if i == H_AT:
                        xa_high(c - 1)
                        for m in range(KD):
                            copy_h((c - 1) * KD + m + 1, m, bank[H_BANKS[m]][:], slice(0, TOK))
                    silu(c, i, False)
                    hid_high(c, i, False)
                if not last:
                    y_high(c + 1, mix_psum)

            act.wait_ge(mix_idx_in, 16)
            act.wait_ge(mixw_zero, 1)
            for j in ACT_MIX:
                load_mix_weight(act, 0, j)
            keep_tile(0)
            y_high(0, acc)
            keep_tile(1)
            keep_tile(2)
            act.wait_ge(small_in, 16 * 3)
            for i in range(TILES):
                silu(0, i, True)
                if i == 0:
                    hid_high(0, i, True)
                for j in TEST_AFTER.get(i, ()):
                    keep_tile(j)
                if i > 0:
                    hid_high(0, i, True)
                if i == 4:
                    act.wait_ge(ab_in, 32)
                    act.activation(a_hi[:], a_stage[:], ACT.Copy).then_inc(w_hi_done, 1)
                if i == 5:
                    act.activation(b_hi[:], b_stage[:], ACT.Copy).then_inc(w_hi_done, 1)
                k = i - 7
                if 0 <= k < KD:
                    if k == 0:
                        act.wait_ge(w_in, 16)
                    act.activation(w_hi[:, k, :], w_stage[:, k, :], ACT.Copy).then_inc(w_hi_done, 1)
            y_high(1, mix_psum)
            with act.Fori(1, CHUNKS - 1) as c:
                chunk(c, False)
            chunk(CHUNKS - 1, True)
            x1_high(CHUNKS - 1)
            xa_high(CHUNKS - 1)
            for n, toks in enumerate(BLOCKS):
                for m in range(KD):
                    copy_h((CHUNKS - 1 + n) * KD + m + 1, m, h_psum(n, m), toks)

        @block.vector
        def _(dve):
            def y_low(c, psum):
                for t in range(KD):
                    dve.wait_ge(y_hi_done, c * KD + t + 1)
                    dve.tensor_tensor(y_lo[:, t, :], psum[t][:], y_hi[:, t, :].bitcast(F32),
                                      ALU.subtract).then_inc(y_lo_done, 1)

            def hidden(c, i, first):
                dve.wait_ge(up_done, c * TILES + i + 1)
                dve.wait_ge(silu_done, c * TILES + i + 1)
                if not (first and i < 2):
                    dve.wait_ge(hid_lo_done, c * TILES + max(i - 1, 0))
                dve.scalar_tensor_tensor(out=hid[:, i % 2, :], in0=bank[2 * (i % 2) + 1][:], scalar=us[:, i:i + 1],
                                         in1=gated[:, i % 2, :], op0=ALU.mult, op1=ALU.mult
                                         ).then_inc(hid_done, 1)

            def x1(c):
                for m in range(KD):
                    dve.wait_ge(acc_done, c * KD + m + 1)
                    dve.wait_ge(xc_in[m], (c + 1) * 16)
                    dve.scalar_tensor_tensor(out=xc[:, m, :], in0=acc[m][:], scalar=ds[:, m:m + 1],
                                             in1=xc[:, m, :], op0=ALU.mult, op1=ALU.add).then_inc(x1_done, 1)

            def xa_mask(c):
                dve.wait_ge(xa_done, c + 1)
                of_batch = mask[:, bass.ds(c * NB, NB)].rearrange("p (b a) -> p b a", a=1).broadcast_to([P, NB, C])
                dve.tensor_tensor(xa[:].rearrange("p (b d) -> p b d", d=C),
                                  bank[0][:].rearrange("p (b d) -> p b d", d=C), of_batch,
                                  ALU.mult).then_inc(xa_masked, 1)

            every = slice(0, TOK)

            def h_max(n, toks):
                dve.wait_ge(h_out, (n + 1) * KD)
                dve.tensor_reduce(amax[:, toks], h[:, :, toks].rearrange("p m n -> p n m"), AX.X, ALU.max,
                                  apply_absolute_value=True).then_inc(amax_done, 1)

            def h_scale(n, toks):
                dve.wait_ge(amax_all_done, n + 1)
                dve.tensor_scalar(scale[:, toks], amax_all[:, toks], EPS, 1.0 / 127.0, ALU.max, ALU.mult
                                  ).then_inc(scale_done, 1)
                dve.wait_ge(scale_done, n + 1)
                dve.reciprocal(rscale[:, toks], scale[:, toks]).then_inc(rscale_done, 1)

            def quantise(n, pair, toks):
                ms = slice(2 * pair, 2 * pair + 2)
                step = 2 * n + pair + 1
                dve.wait_ge(rscale_done, n + 1)
                both = rscale[:, toks].rearrange("p (a n) -> p a n", a=1).broadcast_to([P, 2, toks.stop - toks.start])
                dve.tensor_tensor(h[:, ms, toks], h[:, ms, toks], both, ALU.mult).then_inc(q_scaled, 1)
                dve.wait_ge(q_scaled, step)
                dve.tensor_scalar(h[:, ms, toks], h[:, ms, toks], 127.0, -128.0, ALU.min, ALU.max
                                  ).then_inc(q_clipped, 1)
                dve.wait_ge(q_clipped, step)
                dve.tensor_scalar(q[:, ms, toks], h[:, ms, toks], ROUND, ROUND, ALU.add, ALU.subtract
                                  ).then_inc(q_done, 1)

            def result(n, m, psum, toks):
                dve.wait_ge(ffn_done, n * KD + m + 1)
                dve.scalar_tensor_tensor(out=deq[:, m % 2, toks], in0=psum, scalar=wsum[:, 2:3],
                                         in1=scale[:, toks], op0=ALU.mult, op1=ALU.mult).then_inc(deq_done, 1)
                dve.wait_ge(deq_done, n * KD + m + 1)
                dve.scalar_tensor_tensor(out=xc[:, m, toks], in0=deq[:, m % 2, toks], scalar=bs[:, m:m + 1],
                                         in1=xc[:, m, toks], op0=ALU.add, op1=ALU.add).then_inc(out_done, 1)

            def last_deq(n, m, psum, toks):
                dve.wait_ge(ffn_done, (CHUNKS + n) * KD + m + 1)
                dve.scalar_tensor_tensor(out=h[:, m, toks], in0=psum, scalar=wsum[:, 2:3],
                                         in1=scale[:, toks], op0=ALU.mult, op1=ALU.mult).then_inc(deq_done, 1)

            def test_tile(i):
                low = tile_stage[i % STAGES].bitcast(I32)
                dve.wait_ge(tile_kept, i + 1)
                dve.tensor_scalar(low, low, LOW_BITS, None, ALU.bitwise_and).then_inc(low_done, 1)
                dve.wait_ge(low_done, i + 1)
                dve.tensor_reduce(inexact[:, i:i + 1], low, AX.XY, ALU.max).then_inc(inexact_done, 1)
                dve.wait_ge(inexact_done, i + 1)
                dve.tensor_reduce(inexact_to[:, i:i + 1], inexact[:, 0:i + 1], AX.X, ALU.max).then_inc(tested, 1)

            def chunk(c, last):
                x1(c - 1)
                for i in range(TILES):
                    if i == H_AT:
                        xa_mask(c - 1)
                        h_max(c - 1, every)
                    if i == FFN_AT:
                        for m in range(KD):
                            result(c - 1, m, bank[FFN_BANKS[m]][:], every)
                    hidden(c, i, False)
                    if i == SCALE_AFTER:
                        h_scale(c - 1, every)
                    for pair in range(2):
                        if i == Q_AFTER[pair]:
                            quantise(c - 1, pair, every)
                if not last:
                    y_low(c + 1, mix_psum)

            def make_mask():
                dve.wait_ge(iota_done, 2)
                dve.wait_ge(small_in, 16 * 3)
                dve.tensor_scalar(part_i[:, 1:2], part_i[:, 0:1], RANK.bit_length() - 1, None,
                                  ALU.arith_shift_right).then_inc(mask_step, 1)
                dve.tensor_copy(nums[:], nums_i[:]).then_inc(mask_step, 1)
                dve.tensor_copy(ad_f[:], ad_i[:]).then_inc(mask_step, 1)
                dve.wait_ge(mask_step, 3)
                dve.tensor_copy(own_i[:], part_i[:, 1:2]).then_inc(mask_step, 1)
                dve.wait_ge(mask_step, 4)
                dve.scalar_tensor_tensor(out=own[:], in0=nums[:], scalar=own_i[:, 0:1], in1=scal[:],
                                         op0=ALU.is_equal, op1=ALU.mult).then_inc(mask_step, 1)
                dve.wait_ge(mask_step, 5)
                dve.tensor_reduce(own_s[:], own[:], AX.X, ALU.add).then_inc(mask_step, 1)
                dve.wait_ge(mask_step, 6)
                dve.tensor_scalar(mask[:], ad_f[:], own_i[:, 0:1], own_s[:, 0:1], ALU.is_equal, ALU.mult
                                  ).then_inc(mask_step, 1)
                dve.wait_ge(mask_step, 7)

            dve.memset(mixw[:], 0.0).then_inc(mixw_zero, 1)

            test_tile(0)
            y_low(0, acc)
            test_tile(1)
            test_tile(2)
            dve.wait_ge(small_in, 16 * 3)
            for i in range(TILES):
                hidden(0, i, True)
                for j in TEST_AFTER.get(i, ()):
                    test_tile(j)
                if i == 6:
                    make_mask()
                if i == 8:
                    dve.wait_ge(qw_in, 16)
                    dve.tensor_reduce(wsum[:, 0:1], q_stage[:], AX.XY, ALU.add, apply_absolute_value=True
                                      ).then_inc(wsum_done, 1)
                if i == 9:
                    dve.wait_ge(wsum_all, 1)
                    dve.tensor_scalar(wsum[:, 2:3], wsum[:, 1:2], 1.0 / (D * D), EPS, ALU.mult, ALU.max
                                      ).then_inc(alpha_done, 1)
                    dve.wait_ge(alpha_done, 1)
                    dve.reciprocal(wsum[:, 3:4], wsum[:, 2:3]).then_inc(alpha_done, 1)
                    dve.wait_ge(alpha_done, 2)
                    dve.tensor_scalar(q_stage[:], q_stage[:], wsum[:, 3:4], 1.0, ALU.mult, ALU.min
                                      ).then_inc(qw_step, 1)
            y_low(1, mix_psum)
            dve.wait_ge(qw_step, 1)
            dve.tensor_scalar(q_stage[:], q_stage[:], -1.0, ROUND, ALU.max, ALU.add).then_inc(qw_step, 1)
            dve.wait_ge(qw_step, 2)
            dve.tensor_scalar(qw[:], q_stage[:], -ROUND, None, ALU.add).then_inc(qw_done, 1)

            with dve.Fori(1, CHUNKS - 1) as c:
                chunk(c, False)
            chunk(CHUNKS - 1, True)
            dve.wait_ge(hid_hi_done, CHUNKS * TILES)
            dve.tensor_tensor(hid_lo[:, (TILES - 1) % 2, :], hid[:, (TILES - 1) % 2, :],
                              hid_hi[:, (TILES - 1) % 2, :].bitcast(F32), ALU.subtract).then_inc(hid_lo_last, 1)
            c = CHUNKS - 1
            x1(c)
            for m in (1, 3):
                dve.wait_ge(x1_hi_done, c * KD + m + 1)
                dve.tensor_tensor(x1_lo[:, m, :], xc[:, m, :], x1_hi[:, m, :].bitcast(F32),
                                  ALU.subtract).then_inc(x1_lo_odd, 1)
            xa_mask(c)
            dve.wait_ge(x1_lo_done, CHUNKS * KD - 2)
            dve.wait_ge(x1_lo_odd, 2)
            toks = RESULTS[0]
            for m in range(POOL_TILES):
                dve.tensor_scalar(xc[:, m, toks], xc[:, m, toks], bs[:, m:m + 1], None, ALU.add
                                  ).then_inc(bias_added, 1)
            h_max(c, BLOCKS[0])
            for n, toks in enumerate(BLOCKS):
                h_scale(c + n, toks)
                quantise(c + n, 0, toks)
                if n < len(BLOCKS) - 1:
                    h_max(c + n + 1, BLOCKS[n + 1])
                quantise(c + n, 1, toks)
            for n, toks in enumerate(RESULTS):
                psum = bank_sets[(1, 0)[n]]
                for m in range(KD):
                    last_deq(n, m, psum[m][:, toks], toks)
                for m in range(KD):
                    if n > 0 or m >= POOL_TILES:
                        dve.wait_ge(deq_done, (c + n) * KD + m + 1)
                        dve.scalar_tensor_tensor(out=xc[:, m, toks], in0=h[:, m, toks], scalar=bs[:, m:m + 1],
                                                 in1=xc[:, m, toks], op0=ALU.add, op1=ALU.add
                                                 ).then_inc(out_done, 1)

        @block.gpsimd
        def _(pool):
            def hid_low(c, i, first):
                pool.wait_ge(hid_hi_done, c * TILES + i + 1)
                pool.tensor_tensor(hid_lo[:, i % 2, :], hid[:, i % 2, :], hid_hi[:, i % 2, :].bitcast(F32),
                                   ALU.subtract).then_inc(hid_lo_done, 1)

            def x1_low(c, ms):
                for m in ms:
                    pool.wait_ge(x1_hi_done, c * KD + m + 1)
                    pool.tensor_tensor(x1_lo[:, m, :], xc[:, m, :], x1_hi[:, m, :].bitcast(F32),
                                       ALU.subtract).then_inc(x1_lo_done, 1)

            def xa_low(c):
                pool.wait_ge(xa_hi_done, c + 1)
                pool.tensor_tensor(xa_lo[:], xa[:], xa_hi[:].bitcast(F32), ALU.subtract).then_inc(xa_lo_done, 1)

            def max_all(n, toks):
                pool.wait_ge(wsum_all, 1)
                pool.wait_ge(amax_done, n + 1)
                pool.partition_all_reduce(amax_all[:, toks], amax[:, toks], P, RMAX).then_inc(amax_all_done, 1)

            def flag(i):
                pool.wait_ge(tested, i + 1)
                pool.partition_all_reduce(flags[:, i:i + 1], inexact_to[:, i:i + 1], P, RMAX).then_inc(flag_done, 1)

            def chunk(c, last):
                x1_low(c - 1, range(KD - 1))
                for i in range(TILES - 1 if last else TILES):
                    if i == 1:
                        x1_low(c - 1, (KD - 1,))
                    if i == H_AT:
                        xa_low(c - 1)
                        max_all(c - 1, slice(0, TOK))
                    hid_low(c, i, False)

            pool.memset(silu_warm[:], 0.0).then_inc(warm_zero, 1)
            pool.memset(pe_warm[:], 0.0).then_inc(warm_zero, 1)
            pool.dma_start(vecs[:], vectors).then_inc(small_in, 16)
            pool.dma_start(ad_i[:], adapter_idx.rearrange("(a b) -> a b", a=1).broadcast_to([P, BATCHES])
                          ).then_inc(small_in, 16)
            pool.dma_start(scal[:], scalings.rearrange("(a b) -> a b", a=1).broadcast_to([P, P // RANK])
                          ).then_inc(small_in, 16)
            pool.dma_start(a_stage[:], a_t).then_inc(ab_in, 16)
            pool.dma_start(b_stage[:], b_t).then_inc(ab_in, 16)
            pool.iota(part_i[:, 0:1], pattern=[[0, 1]], base=0, channel_multiplier=1).then_inc(iota_done, 1)
            pool.iota(nums_i[:], pattern=[[1, P // RANK]], base=0, channel_multiplier=0).then_inc(iota_done, 1)
            flag(0)
            flag(1)
            flag(2)
            for i in range(TILES):
                hid_low(0, i, True)
                for j in TEST_AFTER.get(i, ()):
                    flag(j)
                if i == 8:
                    pool.wait_ge(wsum_done, 1)
                    pool.partition_all_reduce(wsum[:, 1:2], wsum[:, 0:1], P, RADD).then_inc(wsum_all, 1)
                if i == 5:
                    pool.wait_ge(w_hi_done, 1)
                    pool.tensor_tensor(a_lo[:], a_stage[:], a_hi[:].bitcast(F32), ALU.subtract).then_inc(w_lo_done, 1)
                if i == 6:
                    pool.wait_ge(w_hi_done, 2)
                    pool.tensor_tensor(b_lo[:], b_stage[:], b_hi[:].bitcast(F32), ALU.subtract).then_inc(w_lo_done, 1)
                k = i - 7
                if 0 <= k < KD:
                    pool.wait_ge(w_hi_done, 2 + k + 1)
                    pool.tensor_tensor(w_lo[:, k, :], w_stage[:, k, :], w_hi[:, k, :].bitcast(F32),
                                       ALU.subtract).then_inc(w_lo_done, 1)
            with pool.Fori(1, CHUNKS - 1) as c:
                chunk(c, False)
            chunk(CHUNKS - 1, True)
            x1_low(CHUNKS - 1, (0, 2))
            xa_low(CHUNKS - 1)
            for n, toks in enumerate(BLOCKS):
                max_all(CHUNKS - 1 + n, toks)
            toks = RESULTS[0]
            for m in range(POOL_TILES):
                pool.wait_ge(bias_added, m + 1)
                pool.wait_ge(deq_done, (CHUNKS - 1) * KD + m + 1)
                pool.tensor_tensor(xc[:, m, toks], h[:, m, toks], xc[:, m, toks], ALU.add
                                   ).then_inc(pool_out, 1)


def kernel(x, itok_B_1_198, itok_B_0_6, L0_cond_weights, L0_ffn_gate_w, L0_ffn_up_w, L0_ffn_down_w, L0_ffn_gate_s,
           L0_ffn_up_s, L0_ffn_down_s, L1_cond_W, L1_cond_A, L1_cond_Bm, L1_cond_scalings, L1_ffn_weight, L1_ffn_bias):
    import numpy as np
    import concourse.bacc as bacc
    from concourse.bass_utils import run_bass_kernel_spmd

    a = np.asarray
    batches, chans, d = x.shape
    kd, tiles = d // P, L0_ffn_gate_w.shape[0] // P

    def rows_in(w):
        return a(w).T.reshape(kd, P, -1).transpose(1, 0, 2)

    def by_tile(w):
        return a(w).reshape(tiles, P, kd, P).transpose(3, 0, 2, 1).reshape(P, tiles, d)

    down = a(L0_ffn_down_w).reshape(kd, P, tiles, P).transpose(3, 2, 0, 1).reshape(P, tiles, d)
    ins = {
        "x_rows": a(x),
        "x_cols": a(x).transpose(2, 0, 1).reshape(d, batches * chans),
        "mix_idx": a(itok_B_1_198),
        "adapter_idx": a(itok_B_0_6),
        "mix_w": a(L0_cond_weights),
        "ffn0_w": np.stack([by_tile(L0_ffn_gate_w), by_tile(L0_ffn_up_w), down], axis=2),
        "vectors": np.concatenate([a(v).reshape(-1, P).T for v in (L0_ffn_gate_s, L0_ffn_up_s, L0_ffn_down_s,
                                                                  L1_ffn_bias)], axis=1),
        "w_t": rows_in(L1_cond_W),
        "a_t": rows_in(a(L1_cond_A).reshape(P, d)),
        "b_t": a(L1_cond_Bm).transpose(0, 2, 1).reshape(P, d),
        "scalings": a(L1_cond_scalings),
        "qw_t": rows_in(L1_ffn_weight),
    }
    nc = bacc.Bacc("TRN2", target_bir_lowering=False, num_devices=1)
    arrays, args = {}, []
    for name, v in ins.items():
        v = np.ascontiguousarray(v)
        arrays[name] = v
        args.append(nc.dram_tensor(name, v.shape, mybir.dt.from_np(v.dtype), kind="ExternalInput").ap())
    args.append(nc.dram_tensor("out", (d, batches * chans), F32, kind="ExternalOutput").ap())
    adaln_ffn_kernel(nc, *args)
    r = run_bass_kernel_spmd(nc, [arrays], core_ids=[0])
    return r.results[0]["out"].reshape(d, batches, chans).transpose(1, 2, 0)
```
